# Optimizing a Trainium2 kernel written in Bass

```python
import numpy as np
import jax
import jax.numpy as jnp

def _softmax(x, axis=-1):
    return jax.nn.softmax(x, axis=axis)

def _gelu(x):
    return jax.nn.gelu(x, approximate=True)

def _silu(x):
    return jax.nn.silu(x)

def _sigmoid(x):
    return jax.nn.sigmoid(x)

def _layernorm(x, axis=-1, eps=1e-05):
    m = jnp.mean(x, axis=axis, keepdims=True)
    v = jnp.var(x, axis=axis, keepdims=True)
    return (x - m) / jnp.sqrt(v + eps)

def _scatter_add(tgt, idx, src, axis=0):
    return tgt.at[idx].add(src)

def _segment_sum(src, seg, n):
    return jax.ops.segment_sum(src, seg, n)
kernel_name = 'mk_adj_preln_d2_adj_r2_9c39d6'

def setup_inputs(seed: int=0):
    np.random.seed(seed)
    _w = jnp.asarray

    def _rec_inputs():
        import jax
        import jax.numpy as jnp
        _gk = jax.random.key(seed)
        x = 7.22e-05 + 1 * jax.random.normal(jax.random.fold_in(_gk, 1), (64, 128, 256), jnp.float32)
        _a = jax.random.bernoulli(jax.random.fold_in(_gk, 2), 0.125, (128, 128))
        adj = _a.astype(jnp.int32)
        return (x, adj)
    x, adj = _rec_inputs()

    def _L0_gnn_setup():
        import jax, jax.numpy as jnp
        import numpy as np
        LEAKY_ALPHA = 0.01
        NEG_INF = -1000000000.0
        LN_EPS = 1e-05

        def _gat_heads(x, adj, W, a):
            O = W.shape[-1]
            Wh = jnp.einsum('bnf,hfo->bhno', x, W)
            f1 = jnp.einsum('bhno,ho->bhn', Wh, a[:, :O])
            f2 = jnp.einsum('bhno,ho->bhn', Wh, a[:, O:])
            e = f1[:, :, :, None] + f2[:, :, None, :]
            e = jnp.where(e > 0, e, LEAKY_ALPHA * e)
            e = jnp.where(adj[None, None] > 0, e, NEG_INF)
            attn = jax.nn.softmax(e, axis=-1)
            return jnp.einsum('bhnm,bhmo->bhno', attn, Wh)
        key = jax.random.key(seed)
        ks = jax.random.split(key, 10)
        B, N, F_in, F_hid, H, F_out, D_ff = (8, 1024, 256, 256, 4, 256, 256)
        s = 0.05
        return {'enc_inputs': jax.random.normal(ks[0], (B, N, F_in), jnp.float32), 'adj': jax.random.randint(ks[1], (N, N), 0, 2, jnp.int32), 'W_heads': jax.random.normal(ks[2], (H, F_in, F_hid), jnp.float32) * s, 'a_heads': jax.random.normal(ks[3], (H, 2 * F_hid), jnp.float32) * s, 'W_out': jax.random.normal(ks[4], (H * F_hid, F_out), jnp.float32) * s, 'a_out': jax.random.normal(ks[5], (2 * F_out,), jnp.float32) * s, 'w1': jax.random.normal(ks[6], (F_out, D_ff), jnp.float32) * s, 'b1': jnp.zeros((D_ff,), jnp.float32), 'w2': jax.random.normal(ks[7], (D_ff, F_out), jnp.float32) * s, 'b2': jnp.zeros((F_out,), jnp.float32), 'ln_gamma': jnp.ones((F_out,), jnp.float32), 'ln_beta': jnp.zeros((F_out,), jnp.float32)}
    _L0_gnn_all = _L0_gnn_setup()
    _L0_gnn_in = {k: v for k, v in _L0_gnn_all.items() if k in ('W_heads', 'a_heads', 'W_out', 'a_out', 'w1', 'b1', 'w2', 'b2', 'ln_gamma', 'ln_beta')}
    del _L0_gnn_all

    def _L1_gnn_setup():
        import jax, jax.numpy as jnp
        import numpy as np
        B, K, DIN, DOUT = (32, 64, 256, 256)
        key = jax.random.key(seed)
        k1, k2, k3, k4 = jax.random.split(key, 4)
        x = jax.random.normal(k1, (B, K, DIN), dtype=jnp.float32)
        adj = jax.random.randint(k2, (K, K), 0, 2, dtype=jnp.int32)
        W = jax.random.normal(k3, (DOUT, 2 * DIN), dtype=jnp.float32) * 0.02
        b = jax.random.normal(k4, (DOUT,), dtype=jnp.float32) * 0.02
        return {'x': x, 'adj': adj, 'W': W, 'b': b}
    _L1_gnn_all = _L1_gnn_setup()
    _L1_gnn_in = {k: v for k, v in _L1_gnn_all.items() if k in ('W', 'b')}
    del _L1_gnn_all
    return {'x': x, 'adj': adj, 'L0_gnn_W_heads': _L0_gnn_in['W_heads'], 'L0_gnn_a_heads': _L0_gnn_in['a_heads'], 'L0_gnn_W_out': _L0_gnn_in['W_out'], 'L0_gnn_a_out': _L0_gnn_in['a_out'], 'L0_gnn_w1': _L0_gnn_in['w1'], 'L0_gnn_b1': _L0_gnn_in['b1'], 'L0_gnn_w2': _L0_gnn_in['w2'], 'L0_gnn_b2': _L0_gnn_in['b2'], 'L0_gnn_ln_gamma': _L0_gnn_in['ln_gamma'], 'L0_gnn_ln_beta': _L0_gnn_in['ln_beta'], 'L1_gnn_W': _L1_gnn_in['W'], 'L1_gnn_b': _L1_gnn_in['b']}

def reference(x, adj, L0_gnn_W_heads, L0_gnn_a_heads, L0_gnn_W_out, L0_gnn_a_out, L0_gnn_w1, L0_gnn_b1, L0_gnn_w2, L0_gnn_b2, L0_gnn_ln_gamma, L0_gnn_ln_beta, L1_gnn_W, L1_gnn_b):
    import jax
    import jax.numpy as jnp

    def _L0_gnn_ref(enc_inputs, adj, W_heads, a_heads, W_out, a_out, w1, b1, w2, b2, ln_gamma, ln_beta):
        import jax, jax.numpy as jnp
        import numpy as np
        LEAKY_ALPHA = 0.01
        NEG_INF = -1000000000.0
        LN_EPS = 1e-05

        def _gat_heads(x, adj, W, a):
            O = W.shape[-1]
            Wh = jnp.einsum('bnf,hfo->bhno', x, W)
            f1 = jnp.einsum('bhno,ho->bhn', Wh, a[:, :O])
            f2 = jnp.einsum('bhno,ho->bhn', Wh, a[:, O:])
            e = f1[:, :, :, None] + f2[:, :, None, :]
            e = jnp.where(e > 0, e, LEAKY_ALPHA * e)
            e = jnp.where(adj[None, None] > 0, e, NEG_INF)
            attn = jax.nn.softmax(e, axis=-1)
            return jnp.einsum('bhnm,bhmo->bhno', attn, Wh)
        B, N, _ = enc_inputs.shape
        h = jax.nn.elu(_gat_heads(enc_inputs, adj, W_heads, a_heads))
        h = jnp.transpose(h, (0, 2, 1, 3)).reshape(B, N, -1)
        out = _gat_heads(h, adj, W_out[None], a_out[None])[:, 0]
        out = jax.nn.elu(out)
        ffn = jnp.maximum(out @ w1 + b1, 0.0) @ w2 + b2
        y = ffn + out
        mu = jnp.mean(y, axis=-1, keepdims=True)
        var = jnp.var(y, axis=-1, keepdims=True)
        return (y - mu) / jnp.sqrt(var + LN_EPS) * ln_gamma + ln_beta

    def _L1_gnn_ref(x, adj, W, b):
        import jax, jax.numpy as jnp
        import numpy as np
        B, K, DIN, DOUT = (32, 64, 256, 256)
        Din = x.shape[-1]
        Wi, Wj = (W[:, :Din], W[:, Din:])
        mi = jnp.einsum('bkd,od->bko', x, Wi)
        mj = jnp.einsum('bkd,od->bko', x, Wj)
        a = adj.astype(x.dtype)
        deg = a.sum(axis=1)
        out = deg[None, :, None] * (mi + b) + jnp.einsum('ij,bjo->bio', a, mj)
        return out
    h = jnp.maximum(_layernorm(x, axis=-1), 0.0)
    x = x + _L0_gnn_ref(h, adj, L0_gnn_W_heads, L0_gnn_a_heads, L0_gnn_W_out, L0_gnn_a_out, L0_gnn_w1, L0_gnn_b1, L0_gnn_w2, L0_gnn_b2, L0_gnn_ln_gamma, L0_gnn_ln_beta)
    h = jnp.maximum(_layernorm(x, axis=-1), 0.0)
    x = x + _L1_gnn_ref(h, adj, L1_gnn_W, L1_gnn_b)
    return x

_drawn_inputs = setup_inputs


def setup_inputs(seed=0):
    import zlib

    import numpy as np

    out = dict(_drawn_inputs(seed))
    spreads = {'L0_gnn_b1': (0.0, 0.1),
     'L0_gnn_b2': (0.0, 0.1),
     'L0_gnn_ln_gamma': (1.0, 0.2),
     'L0_gnn_ln_beta': (0.0, 0.1)}
    factors = {'L0_gnn_a_out': 7.742}
    for name, (base, spread) in spreads.items():
        noise = np.random.default_rng([zlib.crc32(name.encode()), seed]).standard_normal(out[name].shape)
        drawn = base * np.exp(spread * noise) if base else spread * noise
        out[name] = jnp.asarray(drawn.astype(out[name].dtype))
    for name, factor in factors.items():
        out[name] = (out[name] * factor).astype(out[name].dtype)
    return out
```

```python
import numpy as np
from contextlib import ExitStack

import concourse.bass as bass
from concourse import mybir

F32 = mybir.dt.float32
F32R = mybir.dt.float32r
BF16 = mybir.dt.bfloat16
I32 = mybir.dt.int32
ALU = mybir.AluOpType
ACT = mybir.ActivationFunctionType
X = mybir.AxisListType.X

P = 128
BATCH = 64
F = 256
C = F // P
H = 4
K2 = H * C
PAIRS = BATCH // 2
NEG = -1.0e30
EPS = 1e-5
G3 = (32, 64, 96)
WO = F + 2


class Pair:

    def __init__(self, i, c):
        self.i, self.c, self.e = i + c // 2, c % 2, c % 2

    def lagged(self, lag):
        return Pair(self.i, self.c - lag)

    def exists(self):
        return not isinstance(self.i, int) or 0 <= 2 * self.i + self.c < PAIRS

    def count(self, per, k):
        if isinstance(self.i, int):
            return per * (2 * self.i + self.c) + k
        return self.i * (2 * per) + (self.c * per + k)


def build(nc, x, adj, w_heads, a_heads, w_out, a_out, w1, b1, w2, b2, gamma, beta, l1w, l1b, out):
    ctx = ExitStack()
    with ctx:
        def sb(name, shape, dt=F32):
            return ctx.enter_context(nc.sbuf_tensor(name, shape, dt))

        def sem(name):
            return ctx.enter_context(nc.semaphore(name))

        def two(name, shape, dt=F32):
            return [sb(f"{name}{e}", shape, dt) for e in range(2)]

        def same(name, shape, dt=F32):
            return [sb(name, shape, dt)] * 2

        ident = sb("ident", [P, P])
        ident_bf = sb("ident_bf", [P, P], BF16)
        rowsel = sb("rowsel", [P, 8, P], BF16)
        adj_i = sb("adj_i", [P, P], I32)
        adj_f = sb("adj_f", [P, P])
        mask = sb("mask", [P, H, P], BF16)
        deg = sb("deg", [P, 1])
        adj_deg = sb("adj_deg", [P, 2, P])
        lend = sb("lend", [P, 4, 2 * F])
        wh = lend[:, :, :].rearrange("p (c g) (s o) -> p c (g s) o", c=C, s=2)
        lt, x2, x2d, h3 = ([lend[:, k, :].rearrange("p (b o) -> p b o", b=2)] * 2 for k in range(4))
        wh_hi = sb("wh_hi", [P, C, H, F], F32R)
        wh_lo = sb("wh_lo", [P, C, H, F], F32R)
        wo = sb("wo", [P, K2, WO])
        wo_hi = sb("wo_hi", [P, K2, WO], F32R)
        wo_lo = sb("wo_lo", [P, K2, WO], F32R)
        lend2 = sb("lend2", [P, 3, 2, H, P])
        ah_bc = lend2[:, 0:2, :, :, :].rearrange("p x y h m -> p (x y) (h m)")
        zt, zp, zn = (lend2[:, k, :, :, :] for k in range(3))
        ao_bc = sb("ao_bc", [P, 2, F])
        dots = sb("dots", [P, F])
        wa = sb("wa", [P, C, 2, H])
        wa_rep = sb("wa_rep", [P, C, P])
        w1_sb = sb("w1_sb", [P, C, F])
        w2_sb = sb("w2_sb", [P, C, F])
        b1_col = sb("b1_col", [P, C])
        b2_bc = sb("b2_bc", [P, F])
        b2_rest = sb("b2_rest", [P, F])
        b2_parts = sb("b2_parts", [P, F], BF16)
        gamma_bc = sb("gamma_bc", [P, F])
        beta_bc = sb("beta_bc", [P, F])
        l1b_bc = sb("l1b_bc", [P, F])
        deg_bias = sb("deg_bias", [P, F])
        l1w_sb = sb("l1w_sb", [P, C, 2 * F])
        l1w_t = sb("l1w_t", [P, 2, C, F])
        minus_half = sb("minus_half", [P, 2])
        eps = sb("eps", [P, 2])

        xa = two("xa", [P, 2, F])
        xr = two("xr", [P, 2, F])
        a_st, a_mv, a_ve, a_rs, a_nm = (two(n, s) for n, s in (
            ("a_st", [P, 2, 6]), ("a_mv", [P, 2, 2]), ("a_ve", [P, 2]), ("a_rs", [P, 2]), ("a_nm", [P, 2])))
        h = two("h", [P, 2, F])
        h_hi = two("h_hi", [P, 2, F], F32R)
        h_lo = two("h_lo", [P, 2, F], F32R)
        ht = two("ht", [P, C, 2 * P])
        f_parts = two("f_parts", [P, 2 * P], BF16)
        f_rest = two("f_rest", [P, 2 * P])
        zm, zs, zr = (two(n, [P, 2, H]) for n in ("zm", "zs", "zr"))
        at_hi = two("at_hi", [P, 2, H * P], F32R)
        at_lo = two("at_lo", [P, 2, H * P], F32R)
        gh_hi = sb("gh_hi", [P, C, H, 2, P], F32R)
        gh_lo = sb("gh_lo", [P, C, H, 2, P], F32R)
        h2e = two("h2e", [P, C * 2 * P])
        h2v = two("h2v", [P, C * 2 * P])
        h2_hi = sb("h2_hi", [P, H, C, 2 * P], F32R)
        h2_lo = sb("h2_lo", [P, H, C, 2 * P], F32R)
        wh2 = same("wh2", [P, 2, F])
        f2_rep = two("f2_rep", [P, P])
        g_parts = two("g_parts", [P, P], BF16)
        g_rest = two("g_rest", [P, P])
        ym, ys, yr = (two(n, [P, 2]) for n in ("ym", "ys", "yr"))
        yt, yp, yn = (same(n, [P, 2, P]) for n in ("yt", "yp", "yn"))
        a2t = two("a2t", [P, 2, P])
        oe, ov = (same(n, [P, C, 2 * P]) for n in ("oe", "ov"))
        hid = same("hid", [P, C, 2 * P])
        b_st, b_mv, b_ve, b_rs, b_nm = (two(n, s) for n, s in (
            ("b_st", [P, 2, 6]), ("b_mv", [P, 2, 2]), ("b_ve", [P, 2]), ("b_rs", [P, 2]), ("b_nm", [P, 2])))
        c_st, c_mv, c_ve, c_rs, c_nm = (two(n, s) for n, s in (
            ("c_st", [P, 2, 6]), ("c_mv", [P, 2, 2]), ("c_ve", [P, 2]), ("c_rs", [P, 2]), ("c_nm", [P, 2])))
        xb = same("xb", [P, 2, F])
        gd = same("gd", [P, 2, C, 2, P])
        res = two("res", [P, 2, F])

        ps_g = ctx.enter_context(nc.psum_tensor("ps_g", [P, 4, 512], F32))
        ps_x = ctx.enter_context(nc.psum_tensor("ps_x", [P, 2, 512], F32))
        ps_z = ctx.enter_context(nc.psum_tensor("ps_z", [P, 2, 512], F32))

        w_in, c_in, z_ms, z_id, z_sel = sem("w_in"), sem("c_in"), sem("z_ms"), sem("z_id"), sem("z_sel")
        set_dve, set_pe, set_act, set_pool = sem("set_dve"), sem("set_pe"), sem("set_act"), sem("set_pool")
        x_in = [sem(f"x_in{e}") for e in range(2)]
        r_in = [sem(f"r_in{e}") for e in range(2)]
        stored = [sem(f"stored{e}") for e in range(2)]
        S, PER = {}, {}
        for per, names in (
            (1, "a_ve a_rs a_nm h_hi h_lo ht_mm ht_sb f_mm f_c f_r f_m f_l fT_mm fT_c fT_r fT_m fT_l "
                "z2_mm z2_m z2_t z2_d z2_r z2_n a2_mm a2_sb out_mm out_e out_u out_v "
                "b_ve b_rs b_nm lg xb x2 c_ve c_rs c_nm x2d o_mm o_sb"),
            (2, "a_bn a_ag h_sb z_mm z_m z_t z_d z_r z_n at_mm at_hi at_lo wh2_mm wh2_sb wh2_f "
                "hid_mm hid_sb y_mm b_bn b_ag lt c_bn c_ag h3 gd_mm gd_sb"),
            (2, "z2_p"), (2 * H, "z_p"),
            (4, "gh_mm gh_hi gh_lo h2_mm h2_e h2_u h2_v h2_hi h2_lo")):
            for n in names.split():
                S[n], PER[n] = sem("s_" + n), per

        def wait(eng, name, p, k=None, lag=0):
            q = p.lagged(lag)
            if q.exists():
                eng.wait_ge(S[name], q.count(PER[name], PER[name] if k is None else k))

        def half(p, lag=0):
            return (p.lagged(lag).i + 1) * 16

        block = ctx.enter_context(nc.Block())

        def steps(eng, one):
            def at(i, c):
                ps = [Pair(i, c + 1), Pair(i, c), Pair(i, c - 1), Pair(i, c - 2)]
                one(*[q if q.exists() else None for q in ps])
            for t in range(-1, 4):
                at(t // 2, t % 2)
            with eng.Fori(2, PAIRS // 2 - 1) as i:
                for c in range(2):
                    at(i, c)
            for t in range(PAIRS - 2, PAIRS + 2):
                at(t // 2, t % 2)

        SET_WA = 4
        SET_MASK, SET_DEG, SET_DIAG, SET_DB = 5, 6, 7, 8
        SET_B2, SET_WH, SET_WO, SET_ALL = 9, 10, 11, 12

        @block.sync
        def _(sp):
            for c in range(C):
                sp.dma_start(wh[:, c, :, :], w_heads[:, c * P:(c + 1) * P, :].rearrange("h f o -> f h o")).then_inc(w_in, 16)
            sp.dma_start(wo[:, :, 0:F], w_out.rearrange("(k f) o -> f k o", f=P)).then_inc(w_in, 16)
            sp.dma_start(ah_bc[:, :, :], a_heads.partition_broadcast(P)).then_inc(w_in, 16)
            sp.dma_start(ao_bc[:, :, :], a_out.rearrange("(j o) -> j o", j=2).partition_broadcast(P)).then_inc(w_in, 16)
            sp.dma_start(w1_sb[:, :, :], w1.rearrange("(k f) o -> f k o", f=P)).then_inc(w_in, 16)
            sp.dma_start(w2_sb[:, :, :], w2.rearrange("(k f) o -> f k o", f=P)).then_inc(w_in, 16)
            sp.dma_start(l1w_sb[:, :, :], l1w.rearrange("(k o) d -> o k d", o=P)).then_inc(w_in, 16)

            def pair_of(ap, q):
                return ap[bass.ds(q.i * 4 + q.c * 2, 2), :, :].rearrange("b n f -> n b f")

            def one(pl, px, py, pz):
                if pl:
                    wait(sp, "h_sb", pl, lag=2)
                    sp.dma_start(xa[pl.e][:, :, :], pair_of(x, pl)).then_inc(x_in[pl.e], 16)
                if py:
                    wait(sp, "xb", py, lag=2)
                    sp.dma_start(xr[py.e][:, :, :], pair_of(x, py)).then_inc(r_in[py.e], 16)
                if pz:
                    wait(sp, "o_sb", pz)
                    sp.dma_start(pair_of(out, pz), res[pz.e][:, :, :]).then_inc(stored[pz.e], 16)

            steps(sp, one)
            for e in range(2):
                sp.wait_ge(stored[e], PAIRS // 2 * 16)

        @block.gpsimd
        def _(pool):
            pool.dma_start(adj_i[:, :], adj).then_inc(c_in, 16)
            pool.dma_start(b1_col[:, :], b1.rearrange("(k d) -> d k", d=P), allow_slow_non_contiguous=True).then_inc(c_in, 16)
            for dst, src in ((b2_bc, b2), (gamma_bc, gamma), (beta_bc, beta), (l1b_bc, l1b)):
                pool.dma_start(dst[:, :], src.partition_broadcast(P)).then_inc(c_in, 16)
            pool.memset(ident[:, :], 0.0).then_inc(z_ms, 1)
            pool.memset(rowsel[:, :, :], 0.0).then_inc(z_ms, 1)
            pool.memset(minus_half[:, :], -0.5).then_inc(z_ms, 1)
            pool.memset(eps[:, :], EPS).then_inc(z_ms, 1)
            pool.wait_ge(z_ms, 1)
            pool.affine_select(out=ident[:, :], in_=ident[:, :], compare_op=ALU.not_equal, fill=1.0,
                               base=0, pattern=[[-1, P]], channel_multiplier=1).then_inc(z_id, 1)
            pool.wait_ge(z_id, 1)
            pool.tensor_copy(ident_bf[:, :], ident[:, :]).then_inc(z_id, 1)
            pool.wait_ge(z_ms, 2)
            for n, g in enumerate(G3):
                if n:
                    pool.wait_ge(z_sel, n)
                pool.affine_select(out=rowsel[:, :, :], in_=rowsel[:, :, :], compare_op=ALU.not_equal, fill=1.0,
                                   base=-g, pattern=[[-1, 8], [0, P]], channel_multiplier=1).then_inc(z_sel, 1)
            pool.wait_ge(z_ms, 4)

            def rstd(name, p, mv, ve, rs):
                wait(pool, name + "_ag", p)
                pool.tensor_tensor(ve[p.e][:, :], mv[p.e][:, :, 1], eps[:, :], ALU.add).then_inc(S[name + "_ve"], 1)
                wait(pool, name + "_ve", p)
                pool.tensor_tensor(rs[p.e][:, :], ve[p.e][:, :], minus_half[:, :], ALU.pow).then_inc(S[name + "_rs"], 1)

            def h2_low(p, u):
                wait(pool, "h2_hi", p, u + 1)
                pool.tensor_tensor(h2_lo[:, u, :, :].rearrange("p c n -> p (c n)"), h2v[u % 2][:, :],
                                   h2_hi[:, u, :, :].rearrange("p c n -> p (c n)").bitcast(F32), ALU.subtract).then_inc(S["h2_lo"], 1)

            def soft(p, b):
                wait(pool, "z_r", p, b + 1)
                pool.tensor_tensor(zn[:, b, :, :], zp[:, b, :, :],
                                   zr[p.e][:, b, :].unsqueeze(2).broadcast_to([P, H, P]), ALU.mult).then_inc(S["z_n"], 1)

            def one(pl, px, py, pz):
                if pz:
                    if isinstance(pz.i, int) and pz.i == pz.c == 0:
                        pool.wait_ge(c_in, 96)
                    pool.wait_ge(r_in[pz.e], half(pz))
                    pool.tensor_tensor(xb[pz.e][:, :, :], xr[pz.e][:, :, :],
                                       beta_bc[:, :].unsqueeze(1).broadcast_to([P, 2, F]), ALU.add).then_inc(S["xb"], 1)
                if py:
                    h2_low(py, 0)
                    h2_low(py, 1)
                    h2_low(py, 2)
                if px:
                    soft(px, 0)
                if py:
                    h2_low(py, 3)
                if px:
                    soft(px, 1)
                if pz:
                    rstd("b", pz, b_mv, b_ve, b_rs)
                    rstd("c", pz, c_mv, c_ve, c_rs)
                    if isinstance(pz.i, int) and pz.i == pz.c == 0:
                        pool.wait_ge(set_dve, SET_DB)
                    pool.tensor_tensor(x2d[pz.e][:, :, :], x2[pz.e][:, :, :],
                                       deg_bias[:, :].unsqueeze(1).broadcast_to([P, 2, F]), ALU.add).then_inc(S["x2d"], 1)
                if pl:
                    rstd("a", pl, a_mv, a_ve, a_rs)
                    wait(pool, "h_hi", pl)
                    pool.tensor_tensor(h_lo[pl.e][:, :, :], h[pl.e][:, :, :], h_hi[pl.e][:, :, :].bitcast(F32),
                                       ALU.subtract).then_inc(S["h_lo"], 1)

            steps(pool, one)

        @block.vector
        def _(dve):
            own, chain = sem("dve_setup"), [0]

            def after(ins):
                chain[0] += 1
                ins.then_inc(own, 1)
                dve.wait_ge(own, chain[0])

            dve.memset(wa_rep[:, :, :], 0.0).then_inc(set_dve, 1)
            dve.memset(f2_rep[0][:, :], 0.0).then_inc(set_dve, 1)
            dve.memset(f2_rep[1][:, :], 0.0).then_inc(set_dve, 1)
            dve.wait_ge(w_in, 128)
            for c in range(C):
                for hd in range(H):
                    for j in range(2):
                        after(dve.scalar_tensor_tensor(dots[:, :], wh[:, c, hd, :], 1.0, ah_bc[:, hd, j * F:(j + 1) * F],
                                                       ALU.mult, ALU.mult, accum_out=wa[:, c, j, hd:hd + 1]))
            for c in range(C):
                last = dve.tensor_copy(wa_rep[:, c, 32:P].rearrange("p (g r) -> p g r", r=32)[:, :, 0:2 * H],
                                       wa[:, c, :, :].rearrange("p j h -> p (j h)").unsqueeze(1).broadcast_to([P, 3, 2 * H]))
            last.then_inc(set_dve, 1)
            for k in range(K2):
                for j in range(2):
                    after(dve.scalar_tensor_tensor(dots[:, :], wo[:, k, 0:F], 1.0, ao_bc[:, j, :],
                                                   ALU.mult, ALU.mult, accum_out=wo[:, k, F + j:F + j + 1]))
            dve.wait_ge(c_in, 96)
            after(dve.tensor_copy(adj_f[:, :], adj_i[:, :]))
            dve.tensor_scalar(mask[:, :, :], adj_f[:, :].unsqueeze(1).broadcast_to([P, H, P]), 0.0, NEG,
                              ALU.is_le, ALU.mult).then_inc(set_dve, 1)
            after(dve.reduce_sum(deg[:, :], adj_f[:, :], axis=X))
            dve.tensor_scalar(dots[:, 0:1], deg[:, :], 1.0, None, ALU.mult).then_inc(set_dve, 1)
            dve.wait_ge(z_id, 2)
            dve.tensor_scalar(adj_deg[:, 1, :], ident[:, :], deg[:, 0:1], None, ALU.mult).then_inc(set_dve, 1)
            dve.tensor_scalar(deg_bias[:, :], l1b_bc[:, :], deg[:, 0:1], None, ALU.mult).then_inc(set_dve, 1)
            after(dve.tensor_copy(b2_parts[:, :], b2_bc[:, :]))
            after(dve.tensor_tensor(b2_rest[64:P, :], b2_bc[64:P, :], b2_parts[64:P, :], ALU.subtract))
            after(dve.tensor_copy(b2_parts[64:P, :], b2_rest[64:P, :]))
            dve.tensor_tensor(b2_parts[96:P, :], b2_rest[96:P, :], b2_parts[96:P, :], ALU.subtract).then_inc(set_dve, 1)
            after(dve.tensor_copy(wh_hi[:, :, :, :], wh[:, :, :, :]))
            dve.tensor_tensor(wh_lo[:, :, :, :], wh[:, :, :, :], wh_hi[:, :, :, :].bitcast(F32), ALU.subtract).then_inc(set_dve, 1)
            after(dve.tensor_copy(wo_hi[:, :, :], wo[:, :, :]))
            dve.tensor_tensor(wo_lo[:, :, :], wo[:, :, :], wo_hi[:, :, :].bitcast(F32), ALU.subtract).then_inc(set_dve, 1)
            dve.wait_ge(set_pe, 1)
            dve.tensor_copy(adj_deg[:, 0, :], ps_z[:, 0, 0:P])
            for s in range(2):
                for c in range(C):
                    last = dve.tensor_copy(l1w_t[:, s, c, :], ps_g[:, s * C + c, 0:F])
            last.then_inc(set_dve, 1)

            def stats(name, p, src, st, mv):
                for b in range(2):
                    dve.bn_stats(st[p.e][:, b, :], src(b)).then_inc(S[name + "_bn"], 1)
                for b in range(2):
                    wait(dve, name + "_bn", p, b + 1)
                    dve.nop(nofuse=True)
                    dve.bn_aggr(mv[p.e][:, b, :], st[p.e][:, b, :]).then_inc(S[name + "_ag"], 1)

            def shift(name, p, mv, rs, nm):
                wait(dve, name + "_rs", p)
                dve.scalar_tensor_tensor(nm[p.e][:, :], mv[p.e][:, :, 0], -1.0, rs[p.e][:, :], ALU.mult, ALU.mult)\
                   .then_inc(S[name + "_nm"], 1)

            def gh_low(p, u):
                b, c = u // 2, u % 2
                wait(dve, "gh_hi", p, u + 1)
                dve.tensor_tensor(gh_lo[:, c, :, b, :], ps_g[:, (u + 2) % 4, :].rearrange("p (h n) -> p h n", h=H),
                                  gh_hi[:, c, :, b, :].bitcast(F32), ALU.subtract).then_inc(S["gh_lo"], 1)

            def three_parts(name, p, psum, parts, rest, first):
                e = p.e
                if first:
                    wait(dve, name + "_mm", p)
                    dve.tensor_copy(parts[e][:, :], psum).then_inc(S[name + "_c"], 1)
                wait(dve, name + "_c", p)
                dve.tensor_tensor(rest[e][64:P, :], psum[64:P, :], parts[e][64:P, :], ALU.subtract).then_inc(S[name + "_r"], 1)
                wait(dve, name + "_r", p)
                dve.tensor_copy(parts[e][64:P, :], rest[e][64:P, :]).then_inc(S[name + "_m"], 1)
                wait(dve, name + "_m", p)
                dve.tensor_tensor(parts[e][96:P, :], rest[e][96:P, :], parts[e][96:P, :], ALU.subtract).then_inc(S[name + "_l"], 1)

            def elu(p, u):
                i = u % 2
                wait(dve, "h2_e", p, u + 1)
                dve.tensor_scalar(h2e[i][:, :], h2e[i][:, :], 1.0, 0.0, ALU.subtract, ALU.min).then_inc(S["h2_u"], 1)
                wait(dve, "h2_u", p, u + 1)
                if u >= 2:
                    wait(dve, "h2_lo", p, u - 1)
                else:
                    wait(dve, "h2_lo", p, u + 3, lag=1)
                dve.tensor_tensor(h2v[i][:, :], h2e[i][:, :], ps_g[:, (u + 2) % 4, :], ALU.max).then_inc(S["h2_v"], 1)
                wait(dve, "h2_v", p, u + 1)
                dve.tensor_copy(h2_hi[:, u, :, :].rearrange("p c n -> p (c n)"), h2v[i][:, :]).then_inc(S["h2_hi"], 1)

            def soft_leaky(p, b):
                wait(dve, "z_t", p, b + 1)
                dve.scalar_tensor_tensor(zt[:, b, :, :], zt[:, b, :, :], 0.01, zt[:, b, :, :],
                                         ALU.mult, ALU.max).then_inc(S["z_d"], 1)
                wait(dve, "z_d", p, b + 1)
                dve.tensor_reduce(zm[p.e][:, b, :], zt[:, b, :, :], X, ALU.max, negate=True).then_inc(S["z_m"], 1)

            def soft_sum(p, b):
                wait(dve, "z_p", p, H * (b + 1))
                dve.reciprocal(zr[p.e][:, b, :], zs[p.e][:, b, :]).then_inc(S["z_r"], 1)

            def wh2_scores(p, b):
                wait(dve, "wh2_sb", p, b + 1)
                dve.tensor_copy(f2_rep[p.e][:, 32:P].rearrange("p (g r) -> p g r", r=32)[:, :, b:b + 3:2],
                                ps_g[:, 2 + b, F:WO].unsqueeze(1).broadcast_to([P, 3, 2])).then_inc(S["wh2_f"], 1)

            def one(pl, px, py, pz):
                if py:
                    gh_low(py, 0)
                if pz:
                    three_parts("fT", pz, ps_z[:, 0, 0:P], g_parts, g_rest, True)
                if py:
                    gh_low(py, 1)
                    gh_low(py, 2)
                if pz:
                    wait(dve, "z2_t", pz)
                    dve.scalar_tensor_tensor(yt[pz.e][:, :, :], yt[pz.e][:, :, :], 0.01, yt[pz.e][:, :, :],
                                             ALU.mult, ALU.max).then_inc(S["z2_d"], 1)
                    wait(dve, "z2_d", pz)
                    dve.tensor_reduce(ym[pz.e][:, :], yt[pz.e][:, :, :], X, ALU.max, negate=True).then_inc(S["z2_m"], 1)
                if py:
                    gh_low(py, 3)
                if px:
                    three_parts("f", px, ps_x[:, 1, 0:2 * P], f_parts, f_rest, False)
                if pz:
                    wait(dve, "z2_p", pz)
                    dve.reciprocal(yr[pz.e][:, :], ys[pz.e][:, :]).then_inc(S["z2_r"], 1)
                    wait(dve, "z2_r", pz)
                    dve.tensor_tensor(yn[pz.e][:, :, :], yp[pz.e][:, :, :],
                                      yr[pz.e][:, :].unsqueeze(2).broadcast_to([P, 2, P]), ALU.mult).then_inc(S["z2_n"], 1)
                if py:
                    elu(py, 0)
                if px:
                    soft_leaky(px, 0)
                if py:
                    elu(py, 1)
                if pz:
                    wait(dve, "out_e", pz)
                    dve.tensor_scalar(oe[pz.e][:, :, :], oe[pz.e][:, :, :], 1.0, 0.0, ALU.subtract, ALU.min).then_inc(S["out_u"], 1)
                    wait(dve, "out_u", pz)
                    dve.tensor_tensor(ov[pz.e][:, :, :], oe[pz.e][:, :, :],
                                      ps_z[:, 1, :].rearrange("p (c n) -> p c n", c=C), ALU.max).then_inc(S["out_v"], 1)
                if px:
                    soft_leaky(px, 1)
                if py:
                    elu(py, 2)
                if px:
                    soft_sum(px, 0)
                if py:
                    elu(py, 3)
                if px:
                    soft_sum(px, 1)
                if pz:
                    wait(dve, "y_mm", pz)
                    stats("b", pz, lambda b: ps_z[:, 1, b * F:(b + 1) * F], b_st, b_mv)
                    shift("b", pz, b_mv, b_rs, b_nm)
                if py:
                    wh2_scores(py, 0)
                if pz:
                    wait(dve, "lt", pz)
                    dve.tensor_tensor(lt[pz.e][:, :, :], lt[pz.e][:, :, :],
                                      gamma_bc[:, :].unsqueeze(1).broadcast_to([P, 2, F]), ALU.mult).then_inc(S["lg"], 1)
                    wait(dve, "lg", pz)
                    wait(dve, "xb", pz)
                    dve.tensor_tensor(x2[pz.e][:, :, :], lt[pz.e][:, :, :], xb[pz.e][:, :, :], ALU.add).then_inc(S["x2"], 1)
                    wait(dve, "x2", pz)
                    stats("c", pz, lambda b: x2[pz.e][:, b, :], c_st, c_mv)
                if px:
                    for b in range(2):
                        wait(dve, "at_hi", px, b + 1)
                        dve.tensor_tensor(at_lo[px.e][:, b, :], ps_x[:, b, :], at_hi[px.e][:, b, :].bitcast(F32),
                                          ALU.subtract).then_inc(S["at_lo"], 1)
                if pz:
                    shift("c", pz, c_mv, c_rs, c_nm)
                if pl:
                    dve.wait_ge(x_in[pl.e], half(pl))
                    stats("a", pl, lambda b: xa[pl.e][:, b, :], a_st, a_mv)
                    shift("a", pl, a_mv, a_rs, a_nm)
                    wait(dve, "h_sb", pl)
                    dve.tensor_copy(h_hi[pl.e][:, :, :], h[pl.e][:, :, :]).then_inc(S["h_hi"], 1)
                if py:
                    wh2_scores(py, 1)
                if pz:
                    wait(dve, "o_mm", pz)
                    wait(dve, "x2d", pz)
                    if pz.lagged(2).exists():
                        dve.wait_ge(stored[pz.e], half(pz, 2))
                    dve.tensor_tensor(res[pz.e][:, :, :], x2d[pz.e][:, :, :],
                                      ps_z[:, 0, :].rearrange("p (b o) -> p b o", b=2), ALU.add).then_inc(S["o_sb"], 1)

            steps(dve, one)

        @block.scalar
        def _(act):
            act.wait_ge(c_in, 96)

            def gh_high(p, u):
                b, c = u // 2, u % 2
                wait(act, "gh_mm", p, u + 1)
                act.activation(gh_hi[:, c, :, b, :], ps_g[:, (u + 2) % 4, :].rearrange("p (h n) -> p h n", h=H),
                               ACT.Copy).then_inc(S["gh_hi"], 1)

            def elu_exp(p, u):
                if u >= 2:
                    wait(act, "h2_v", p, u - 1)
                else:
                    wait(act, "h2_v", p, u + 3, lag=1)
                wait(act, "h2_mm", p, u + 1)
                act.activation(h2e[u % 2][:, :], ps_g[:, (u + 2) % 4, :], ACT.Exp).then_inc(S["h2_e"], 1)

            def score_copy(p, b):
                wait(act, "z_mm", p, b + 1)
                act.activation(zt[:, b, :, :], ps_x[:, b, :].rearrange("p (h m) -> p h m", h=H), ACT.Copy)\
                   .then_inc(S["z_t"], 1)

            def soft_exp(p, b):
                wait(act, "z_d", p, b + 1)
                wait(act, "z_m", p, b + 1)
                for hd in range(H):
                    act.activation(zp[:, b, hd, :], zt[:, b, hd, :], ACT.Exp, bias=zm[p.e][:, b, hd:hd + 1],
                                   accum_out=zs[p.e][:, b, hd:hd + 1]).then_inc(S["z_p"], 1)

            def wh2_copy(p, b):
                wait(act, "wh2_mm", p, b + 1)
                act.activation(wh2[p.e][:, b, :], ps_g[:, 2 + b, 0:F], ACT.Copy).then_inc(S["wh2_sb"], 1)

            def normal(name, p, dst, src, rs, nm, func, done):
                wait(act, name + "_nm", p)
                for b in range(2):
                    act.activation(dst[p.e][:, b, :], src(b), func, bias=nm[p.e][:, b:b + 1],
                                   scale=rs[p.e][:, b:b + 1]).then_inc(S[done], 1)

            def one(pl, px, py, pz):
                if py:
                    gh_high(py, 0)
                    gh_high(py, 1)
                if px:
                    wait(act, "ht_mm", px)
                    act.activation(ht[px.e][:, :, :], ps_x[:, 0, :].rearrange("p (c n) -> p c n", c=C), ACT.Copy)\
                       .then_inc(S["ht_sb"], 1)
                if py:
                    gh_high(py, 2)
                if pz:
                    wait(act, "z2_mm", pz)
                    act.activation(yt[pz.e][:, :, :], ps_z[:, 1, 0:2 * P].rearrange("p (b m) -> p b m", b=2),
                                   ACT.Copy).then_inc(S["z2_t"], 1)
                if py:
                    gh_high(py, 3)
                if px:
                    wait(act, "f_mm", px)
                    act.activation(f_parts[px.e][:, :], ps_x[:, 1, 0:2 * P], ACT.Copy).then_inc(S["f_c"], 1)
                if pz:
                    wait(act, "z2_d", pz)
                    wait(act, "z2_m", pz)
                    for b in range(2):
                        act.activation(yp[pz.e][:, b, :], yt[pz.e][:, b, :], ACT.Exp, bias=ym[pz.e][:, b:b + 1],
                                       accum_out=ys[pz.e][:, b:b + 1]).then_inc(S["z2_p"], 1)
                if py:
                    elu_exp(py, 0)
                if pz:
                    wait(act, "a2_mm", pz)
                    act.activation(a2t[pz.e][:, :, :], ps_z[:, 0, 0:2 * P].rearrange("p (b m) -> p b m", b=2), ACT.Copy)\
                       .then_inc(S["a2_sb"], 1)
                if px:
                    score_copy(px, 0)
                    score_copy(px, 1)
                if py:
                    elu_exp(py, 1)
                if pz:
                    wait(act, "out_mm", pz)
                    act.activation(oe[pz.e][:, :, :], ps_z[:, 1, :].rearrange("p (c n) -> p c n", c=C), ACT.Exp)\
                       .then_inc(S["out_e"], 1)
                if px:
                    soft_exp(px, 0)
                if py:
                    elu_exp(py, 2)
                if px:
                    soft_exp(px, 1)
                if pz:
                    for c in range(C):
                        wait(act, "hid_mm", pz)
                        act.activation(hid[pz.e][:, c, :], ps_z[:, 0, c * 2 * P:(c + 1) * 2 * P], ACT.Relu,
                                       bias=b1_col[:, c:c + 1]).then_inc(S["hid_sb"], 1)
                if py:
                    elu_exp(py, 3)
                if pz:
                    normal("b", pz, lt, lambda b: ps_z[:, 1, b * F:(b + 1) * F], b_rs, b_nm, ACT.Identity, "lt")
                if py:
                    wh2_copy(py, 0)
                if px:
                    for b in range(2):
                        wait(act, "at_mm", px, b + 1)
                        act.activation(at_hi[px.e][:, b, :], ps_x[:, b, :], ACT.Copy).then_inc(S["at_hi"], 1)
                if pz:
                    normal("c", pz, h3, lambda b: x2[pz.e][:, b, :], c_rs, c_nm, ACT.Relu, "h3")
                if pl:
                    normal("a", pl, h, lambda b: xa[pl.e][:, b, :], a_rs, a_nm, ACT.Relu, "h_sb")
                if pz:
                    for b in range(2):
                        wait(act, "gd_mm", pz, b + 1)
                        act.activation(gd[pz.e][:, b, :, :, :], ps_z[:, b, :].rearrange("p (c s n) -> p c s n", c=C, s=2),
                                       ACT.Copy).then_inc(S["gd_sb"], 1)
                if py:
                    wh2_copy(py, 1)

            steps(act, one)

        @block.tensor
        def _(pe):
            pe.wait_ge(w_in, 128)
            pe.wait_ge(z_id, 2)
            pe.wait_ge(z_sel, 3)
            pe.wait_ge(set_dve, SET_DEG)
            pe.transpose(ps_z[:, 0, 0:P], adj_f[:, :], ident[:, :])
            for s in range(2):
                for c in range(C):
                    for k in range(C):
                        last = pe.transpose(ps_g[:, s * C + c, k * P:(k + 1) * P],
                                            l1w_sb[:, k, s * F + c * P:s * F + (c + 1) * P], ident[:, :])
            last.then_inc(set_pe, 1)
            pe.wait_ge(set_dve, SET_ALL)

            def mm(out_, lhs, rhs, start, stop):
                return pe.matmul(out_, lhs, rhs, start=start, stop=stop)

            def three(out_, lhs, rhs, first, last):
                mm(out_, lhs[0], rhs[0], first, False)
                mm(out_, lhs[0], rhs[1], False, False)
                return mm(out_, lhs[1], rhs[0], False, last)

            def gh_unit(p, u):
                b, c = u // 2, u % 2
                bank = (u + 2) % 4
                if u == 0:
                    wait(pe, "h_lo", p)
                    wait(pe, "at_lo", p)
                if u < 2:
                    wait(pe, "wh2_sb", p, u + 1, lag=1)
                    wait(pe, "wh2_f", p, u + 1, lag=1)
                else:
                    wait(pe, "h2_v", p, u + 1, lag=1)
                cols = slice(c * P, (c + 1) * P)
                three(ps_g[:, bank, :], (h_hi[p.e][:, b, cols], h_lo[p.e][:, b, cols]),
                      (at_hi[p.e][:, b, :], at_lo[p.e][:, b, :]), True, True).then_inc(S["gh_mm"], 1)

            def h2_unit(p, u):
                bank = (u + 2) % 4
                if u == 0:
                    wait(pe, "gh_lo", p)
                for oc in range(C):
                    for c in range(C):
                        cols = slice(oc * P, (oc + 1) * P)
                        last = three(ps_g[:, bank, oc * 2 * P:(oc + 1) * 2 * P],
                                     (wh_hi[:, c, u, cols], wh_lo[:, c, u, cols]),
                                     (gh_hi[:, c, u, :, :].rearrange("p b n -> p (b n)"),
                                      gh_lo[:, c, u, :, :].rearrange("p b n -> p (b n)")), c == 0, c == C - 1)
                last.then_inc(S["h2_mm"], 1)

            def wh2_part(p, b, k0, k1):
                if k0 == 0:
                    wait(pe, "h2_v", p, b + 1)
                rows = slice(b * P, (b + 1) * P)
                for k in range(k0, k1):
                    if b == 0 and k % C == 0:
                        wait(pe, "h2_lo", p, k // C + 1)
                    last = three(ps_g[:, 2 + b, 0:WO], (h2_hi[:, k // C, k % C, rows], h2_lo[:, k // C, k % C, rows]),
                                 (wo_hi[:, k, :], wo_lo[:, k, :]), k == 0, k == K2 - 1)
                if k1 == K2:
                    last.then_inc(S["wh2_mm"], 1)

            def h_transposes(p):
                wait(pe, "h_sb", p)
                wait(pe, "at_lo", p, 1, lag=1)
                for c in range(C):
                    for b in range(2):
                        last = pe.transpose(ps_x[:, 0, (c * 2 + b) * P:(c * 2 + b + 1) * P],
                                            h[p.e][:, b, c * P:(c + 1) * P], ident[:, :])
                last.then_inc(S["ht_mm"], 1)

            def score_rows(p):
                wait(pe, "ht_sb", p)
                wait(pe, "at_lo", p, 2, lag=1)
                for c in range(C):
                    last = mm(ps_x[:, 1, 0:2 * P], wa_rep[:, c, :], ht[p.e][:, c, :], c == 0, c == C - 1)
                last.then_inc(S["f_mm"], 1)

            def scores(p):
                wait(pe, "f_l", p)
                for b in range(2):
                    rows = f_parts[p.e][:, b * P:(b + 1) * P]
                    mm(ps_x[:, b, :], ident_bf[:, :], mask[:, :, :].rearrange("p h m -> p (h m)"), True, False)
                    mm(ps_x[:, b, :], rows, rowsel[:, 0:H, :].rearrange("p h m -> p (h m)"), False, False)
                    for hd in range(H):
                        last = mm(ps_x[:, b, hd * P:(hd + 1) * P], rowsel[:, H + hd, :], rows, False, hd == H - 1)
                    last.then_inc(S["z_mm"], 1)

            def prob_transposes(p, b):
                wait(pe, "z_n", p, b + 1)
                for hd in range(H):
                    last = pe.transpose(ps_x[:, b, hd * P:(hd + 1) * P], zn[:, b, hd, :], ident[:, :])
                last.then_inc(S["at_mm"], 1)

            def z_scores_t(p):
                wait(pe, "wh2_f", p)
                wait(pe, "o_sb", p, lag=1)
                pe.transpose(ps_z[:, 0, 0:P], f2_rep[p.e][:, :], ident[:, :]).then_inc(S["fT_mm"], 1)

            def z_scores(p):
                wait(pe, "fT_l", p)
                mm(ps_z[:, 1, 0:2 * P], ident_bf[:, :], mask[:, 0:2, :].rearrange("p b m -> p (b m)"), True, False)
                mm(ps_z[:, 1, 0:2 * P], g_parts[p.e][:, :], rowsel[:, 0:2, :].rearrange("p b m -> p (b m)"), False, False)
                for b in range(2):
                    last = mm(ps_z[:, 1, b * P:(b + 1) * P], rowsel[:, 2 + b, :], g_parts[p.e][:, :], False, b == 1)
                last.then_inc(S["z2_mm"], 1)

            def z_probs_t(p):
                wait(pe, "z2_n", p)
                for b in range(2):
                    last = pe.transpose(ps_z[:, 0, b * P:(b + 1) * P], yn[p.e][:, b, :], ident[:, :])
                last.then_inc(S["a2_mm"], 1)

            def z_out(p):
                wait(pe, "a2_sb", p)
                wait(pe, "wh2_sb", p)
                for oc in range(C):
                    for b in range(2):
                        last = mm(ps_z[:, 1, (oc * 2 + b) * P:(oc * 2 + b + 1) * P],
                                  wh2[p.e][:, b, oc * P:(oc + 1) * P], a2t[p.e][:, b, :], True, True)
                last.then_inc(S["out_mm"], 1)

            def z_hidden(p):
                wait(pe, "out_v", p)
                for dc in range(C):
                    for c in range(C):
                        last = mm(ps_z[:, 0, dc * 2 * P:(dc + 1) * 2 * P], w1_sb[:, c, dc * P:(dc + 1) * P],
                                  ov[p.e][:, c, :], c == 0, c == C - 1)
                    last.then_inc(S["hid_mm"], 1)

            def z_ffn(p):
                wait(pe, "hid_sb", p)
                for b in range(2):
                    rows = slice(b * P, (b + 1) * P)
                    mm(ps_z[:, 1, b * F:(b + 1) * F], rowsel[:, 0, :], b2_parts[:, :], True, False)
                    for c in range(C):
                        mm(ps_z[:, 1, b * F + c * P:b * F + (c + 1) * P], ov[p.e][:, c, rows], ident[:, :], False, False)
                    for c in range(C):
                        last = mm(ps_z[:, 1, b * F:(b + 1) * F], hid[p.e][:, c, rows], w2_sb[:, c, :], False, c == C - 1)
                    last.then_inc(S["y_mm"], 1)

            def z_gather(p):
                for b in range(2):
                    wait(pe, "h3", p, b + 1)
                    for c in range(C):
                        last = mm(ps_z[:, b, c * F:(c + 1) * F], h3[p.e][:, b, c * P:(c + 1) * P],
                                  adj_deg[:, :, :].rearrange("p s n -> p (s n)"), True, True)
                    last.then_inc(S["gd_mm"], 1)

            def z_last(p):
                wait(pe, "gd_sb", p)
                for b in range(2):
                    for s in range(2):
                        for c in range(C):
                            last = mm(ps_z[:, 0, b * F:(b + 1) * F], gd[p.e][:, b, c, s, :], l1w_t[:, 1 - s, c, :],
                                      s == 0 and c == 0, s == 1 and c == C - 1)
                last.then_inc(S["o_mm"], 1)

            def one(pl, px, py, pz):
                if py:
                    gh_unit(py, 0)
                if pz:
                    z_scores_t(pz)
                if py:
                    gh_unit(py, 1)
                if px:
                    h_transposes(px)
                if py:
                    gh_unit(py, 2)
                if pz:
                    z_scores(pz)
                if py:
                    gh_unit(py, 3)
                if px:
                    score_rows(px)
                if py:
                    h2_unit(py, 0)
                if pz:
                    z_probs_t(pz)
                if px:
                    scores(px)
                if py:
                    h2_unit(py, 1)
                if pz:
                    z_out(pz)
                if py:
                    h2_unit(py, 2)
                if pz:
                    z_hidden(pz)
                if py:
                    h2_unit(py, 3)
                if pz:
                    z_ffn(pz)
                if py:
                    wh2_part(py, 0, 0, K2)
                if px:
                    prob_transposes(px, 0)
                    prob_transposes(px, 1)
                if py:
                    wh2_part(py, 1, 0, K2 // 2)
                if pz:
                    z_gather(pz)
                if py:
                    wh2_part(py, 1, K2 // 2, K2)
                if pz:
                    z_last(pz)

            steps(pe, one)


NAMES = ["x", "adj", "L0_gnn_W_heads", "L0_gnn_a_heads", "L0_gnn_W_out", "L0_gnn_a_out", "L0_gnn_w1", "L0_gnn_b1",
         "L0_gnn_w2", "L0_gnn_b2", "L0_gnn_ln_gamma", "L0_gnn_ln_beta", "L1_gnn_W", "L1_gnn_b"]


def kernel(**inputs):
    import concourse.bacc as bacc
    from concourse.bass_utils import run_bass_kernel_spmd

    nc = bacc.Bacc("TRN2", target_bir_lowering=False, num_devices=1)
    arrays, args = {}, []
    for name in NAMES:
        a = np.ascontiguousarray(inputs[name])
        arrays[f"in_{name}"] = a
        args.append(nc.dram_tensor(f"in_{name}", a.shape, mybir.dt.from_np(a.dtype), kind="ExternalInput").ap())
    args.append(nc.dram_tensor("out_0", (BATCH, P, F), F32, kind="ExternalOutput").ap())
    build(nc, *args)
    r = run_bass_kernel_spmd(nc, [arrays], core_ids=[0])
    return r.results[0]["out_0"]
```

```python
import numpy as np
from contextlib import ExitStack

import concourse.bass as bass
from concourse import mybir

F32 = mybir.dt.float32
F32R = mybir.dt.float32r
BF16 = mybir.dt.bfloat16
I32 = mybir.dt.int32
ALU = mybir.AluOpType
ACT = mybir.ActivationFunctionType
X = mybir.AxisListType.X

P = 128
BATCH = 64
F = 256
C = F // P
H = 4
K2 = H * C
PAIRS = BATCH // 2
NEG = -1.0e30
EPS = 1e-5
G3 = (32, 64, 96)
STAGES = 6
WO = F + 2


class Pair:

    def __init__(self, i, c):
        self.i, self.c, self.e = i + c // 2, c % 2, c % 2

    def lagged(self, lag):
        return Pair(self.i, self.c - lag)

    def exists(self):
        return not isinstance(self.i, int) or 0 <= 2 * self.i + self.c < PAIRS

    def is_first(self):
        return isinstance(self.i, int) and 2 * self.i + self.c == 0

    def count(self, per, k):
        if isinstance(self.i, int):
            return per * (2 * self.i + self.c) + k
        return self.i * (2 * per) + (self.c * per + k)


def build(nc, x, adj, w_heads, a_heads, w_out, a_out, w1, b1, w2, b2, gamma, beta, l1w, l1b, out):
    ctx = ExitStack()
    with ctx:
        def sb(name, shape, dt=F32):
            return ctx.enter_context(nc.sbuf_tensor(name, shape, dt))

        def sem(name):
            return ctx.enter_context(nc.semaphore(name))

        def two(name, shape, dt=F32):
            return [sb(f"{name}{e}", shape, dt) for e in range(2)]

        def same(name, shape, dt=F32):
            return [sb(name, shape, dt)] * 2

        ident = sb("ident", [P, P])
        ident_bf = sb("ident_bf", [P, P], BF16)
        rowsel = sb("rowsel", [P, 8, P], BF16)
        adj_i = sb("adj_i", [P, P], I32)
        adj_f = sb("adj_f", [P, P])
        mask = sb("mask", [P, H, P], BF16)
        deg = sb("deg", [P, 1])
        adj_deg = sb("adj_deg", [P, 2, P], F32R)
        lend = sb("lend", [P, 4, 2 * F])
        wh = lend[:, :, :].rearrange("p (c g) (s o) -> p c (g s) o", c=C, s=2)
        lt, x2, x2d, h3 = ([lend[:, k, :].rearrange("p (b o) -> p b o", b=2)] * 2 for k in range(4))
        wh_hi = sb("wh_hi", [P, C, H, F], F32R)
        wh_lo = sb("wh_lo", [P, C, H, F], F32R)
        lend3 = sb("lend3", [P, K2 * WO])
        wo = lend3[:, :].rearrange("p (k o) -> p k o", k=K2)
        h2e, h2v = ([lend3[:, (2 * j + e) * C * 2 * P:(2 * j + e + 1) * C * 2 * P] for e in range(2)] for j in range(2))
        wo_hi = sb("wo_hi", [P, K2, WO], F32R)
        wo_lo = sb("wo_lo", [P, K2, WO], F32R)
        lend2 = sb("lend2", [P, 3, 2, H, P])
        ah_bc = lend2[:, 0:2, :, :, :].rearrange("p x y h m -> p (x y) (h m)")
        zt, zp, zn = (lend2[:, k, :, :, :] for k in range(3))
        ao_bc = sb("ao_bc", [P, 2, F])
        wa = sb("wa", [P, C, 2, H])
        wa_rep = sb("wa_rep", [P, C, P])
        w1_sb = sb("w1_sb", [P, C, F])
        w2_sb = sb("w2_sb", [P, C, F])
        b1_col = sb("b1_col", [P, C])
        b2_bc = sb("b2_bc", [P, F])
        b2_rest = sb("b2_rest", [P, F])
        b2_parts = sb("b2_parts", [P, F], BF16)
        gamma_bc = sb("gamma_bc", [P, F])
        beta_bc = sb("beta_bc", [P, F])
        l1b_bc = sb("l1b_bc", [P, F])
        deg_bias = sb("deg_bias", [P, F])
        l1w_sb = sb("l1w_sb", [P, C, 2 * F])
        l1w_hi = sb("l1w_hi", [P, 2, C, F], F32R)
        l1w_lo = sb("l1w_lo", [P, 2, C, F], F32R)
        minus_half = sb("minus_half", [P, 2])
        eps = sb("eps", [P, 2])

        xa = two("xa", [P, 2, F])
        xr = two("xr", [P, 2, F])
        a_st, a_mv, a_ve, a_rs, a_nm = (two(n, s) for n, s in (
            ("a_st", [P, 2, 6]), ("a_mv", [P, 2, 2]), ("a_ve", [P, 2]), ("a_rs", [P, 2]), ("a_nm", [P, 2])))
        h = two("h", [P, 2, F])
        h_hi = two("h_hi", [P, 2, F], F32R)
        h_lo = two("h_lo", [P, 2, F], F32R)
        ht = same("ht", [P, C, 2 * P])
        f_parts = same("f_parts", [P, 2 * P], BF16)
        f_rest = same("f_rest", [P, 2 * P])
        zm, zs, zr = (two(n, [P, 2, H]) for n in ("zm", "zs", "zr"))
        at_hi = two("at_hi", [P, 2, H * P], F32R)
        at_lo = two("at_lo", [P, 2, H * P], F32R)
        gh_hi = sb("gh_hi", [P, C, H, 2, P], F32R)
        gh_lo = sb("gh_lo", [P, C, H, 2, P], F32R)
        h2_hi = sb("h2_hi", [P, H, C, 2 * P], F32R)
        h2_lo = sb("h2_lo", [P, H, C, 2 * P], F32R)
        wh2 = same("wh2", [P, 2, F])
        f2_rep = two("f2_rep", [P, P])
        g_parts = two("g_parts", [P, P], BF16)
        g_rest = two("g_rest", [P, P])
        ym, ys, yr = (two(n, [P, 2]) for n in ("ym", "ys", "yr"))
        yt, yp, yn = (same(n, [P, 2, P]) for n in ("yt", "yp", "yn"))
        a2t = two("a2t", [P, 2, P])
        oe, ov = (same(n, [P, C, 2 * P]) for n in ("oe", "ov"))
        hid = same("hid", [P, C, 2 * P])
        b_st, b_mv, b_ve, b_rs, b_nm = (two(n, s) for n, s in (
            ("b_st", [P, 2, 6]), ("b_mv", [P, 2, 2]), ("b_ve", [P, 2]), ("b_rs", [P, 2]), ("b_nm", [P, 2])))
        c_st, c_mv, c_ve, c_rs, c_nm = (two(n, s) for n, s in (
            ("c_st", [P, 2, 6]), ("c_mv", [P, 2, 2]), ("c_ve", [P, 2]), ("c_rs", [P, 2]), ("c_nm", [P, 2])))
        xb = same("xb", [P, 2, F])
        h3_hi = sb("h3_hi", [P, 2, F], F32R)
        h3_lo = sb("h3_lo", [P, 2, F], F32R)
        gd_hi = sb("gd_hi", [P, 2, C, 2, P], F32R)
        gd_lo = sb("gd_lo", [P, 2, C, 2, P], F32R)
        res = two("res", [P, 2, F])

        ps_g = ctx.enter_context(nc.psum_tensor("ps_g", [P, 4, 512], F32))
        ps_x = ctx.enter_context(nc.psum_tensor("ps_x", [P, 2, 512], F32))
        ps_z = ctx.enter_context(nc.psum_tensor("ps_z", [P, 2, 512], F32))

        heads_in, out_in, ffn_in, last_in = sem("heads_in"), sem("out_in"), sem("ffn_in"), sem("last_in")
        dotted = sem("dotted")
        adj_in, c_in, z_ms, z_id, z_sel = sem("adj_in"), sem("c_in"), sem("z_ms"), sem("z_id"), sem("z_sel")
        set_dve, set_pe, set_act, set_pool = sem("set_dve"), sem("set_pe"), sem("set_act"), sem("set_pool")
        x_in = [sem(f"x_in{e}") for e in range(2)]
        r_in = [sem(f"r_in{e}") for e in range(2)]
        stored = [sem(f"stored{e}") for e in range(2)]
        S, PER = {}, {}
        for per, names in (
            (1, "a_ve a_rs a_nm h_hi h_lo ht_mm ht_sb f_mm f_c f_r f_m f_l fT_mm fT_c fT_r fT_m fT_l "
                "z2_mm z2_m z2_t z2_d z2_r z2_n a2_mm a2_sb out_mm out_e out_u out_v "
                "b_ve b_rs b_nm lg xb x2 c_ve c_rs c_nm x2d h3_hi h3_lo o_mm o_sb"),
            (2, "a_bn a_ag h_sb z_mm z_m z_t z_d z_r z_n at_mm at_hi at_lo wh2_mm wh2_sb wh2_f "
                "hid_mm hid_sb y_mm b_bn b_ag lt c_bn c_ag h3 gd_mm gd_hi gd_lo"),
            (2, "z2_p"), (2 * H, "z_p"),
            (4, "gh_mm gh_hi gh_lo h2_mm h2_e h2_u h2_v h2_hi h2_lo")):
            for n in names.split():
                S[n], PER[n] = sem("s_" + n), per

        def wait(eng, name, p, k=None, lag=0):
            q = p.lagged(lag)
            if q.exists():
                eng.wait_ge(S[name], q.count(PER[name], PER[name] if k is None else k))

        def half(p, lag=0):
            return (p.lagged(lag).i + 1) * 16

        block = ctx.enter_context(nc.Block())

        def steps(eng, one, between=()):
            def at(i, c):
                pairs = [Pair(i, c - k) for k in range(STAGES)]
                one([q if q.exists() else None for q in pairs])
            fill = STAGES + STAGES % 2 + 2
            for t in range(fill):
                at(t // 2, t % 2)
                if t < len(between):
                    between[t]()
            with eng.Fori(fill // 2, PAIRS // 2) as i:
                for c in range(2):
                    at(i, c)
            for t in range(PAIRS, PAIRS + STAGES - 1):
                at(t // 2, t % 2)

        DVE_ADJ, DVE_MASK, DVE_WA, DVE_WH, DVE_DEG, DVE_B2, DVE_LAST = 4, 5, 6, 7, 8, 9, 10
        DOTS_HEADS, DOTS_ALL = 2 * C * H, 2 * C * H + 2 * K2
        ACT_WH, ACT_WO, ACT_LAST = 1, 2, 4
        POOL_WO = 1

        @block.sync
        def _(sp):
            for c in range(C):
                sp.dma_start(wh[:, c, :, :], w_heads[:, c * P:(c + 1) * P, :].rearrange("h f o -> f h o")).then_inc(heads_in, 16)
            sp.dma_start(ah_bc[:, :, :], a_heads.partition_broadcast(P)).then_inc(heads_in, 16)

            def load_later_weights():
                sp.dma_start(wo[:, :, 0:F], w_out.rearrange("(k f) o -> f k o", f=P)).then_inc(out_in, 16)
                sp.dma_start(ao_bc[:, :, :], a_out.rearrange("(j o) -> j o", j=2).partition_broadcast(P)).then_inc(out_in, 16)
                sp.dma_start(l1w_sb[:, :, :], l1w.rearrange("(k o) d -> o k d", o=P)).then_inc(last_in, 16)
                sp.dma_start(w1_sb[:, :, :], w1.rearrange("(k f) o -> f k o", f=P)).then_inc(ffn_in, 16)
                sp.dma_start(w2_sb[:, :, :], w2.rearrange("(k f) o -> f k o", f=P)).then_inc(ffn_in, 16)

            def pair_of(ap, q):
                return ap[bass.ds(q.i * 4 + q.c * 2, 2), :, :].rearrange("b n f -> n b f")

            def load_x(p):
                wait(sp, "h_sb", p, lag=2)
                sp.dma_start(xa[p.e][:, :, :], pair_of(x, p)).then_inc(x_in[p.e], 16)

            def load_residual(p):
                wait(sp, "xb", p, lag=2)
                sp.dma_start(xr[p.e][:, :, :], pair_of(x, p)).then_inc(r_in[p.e], 16)

            def store(p):
                wait(sp, "o_sb", p)
                sp.dma_start(pair_of(out, p), res[p.e][:, :, :]).then_inc(stored[p.e], 16)

            def one(pairs):
                if p := pairs[5]:
                    store(p)
                if p := pairs[3]:
                    load_residual(p)
                if p := pairs[0]:
                    load_x(p)
            steps(sp, one, [load_later_weights])
            for e in range(2):
                sp.wait_ge(stored[e], PAIRS // 2 * 16)

        @block.gpsimd
        def _(pool):
            pool.dma_start(adj_i[:, :], adj).then_inc(adj_in, 16)
            pool.dma_start(b1_col[:, :], b1.rearrange("(k d) -> d k", d=P), allow_slow_non_contiguous=True).then_inc(c_in, 16)
            for dst, src in ((b2_bc, b2), (gamma_bc, gamma), (beta_bc, beta), (l1b_bc, l1b)):
                pool.dma_start(dst[:, :], src.partition_broadcast(P)).then_inc(c_in, 16)
            pool.memset(ident[:, :], 0.0).then_inc(z_ms, 1)
            pool.memset(rowsel[:, :, :], 0.0).then_inc(z_ms, 1)
            pool.memset(minus_half[:, :], -0.5).then_inc(z_ms, 1)
            pool.memset(eps[:, :], EPS).then_inc(z_ms, 1)
            pool.wait_ge(z_ms, 1)
            pool.affine_select(out=ident[:, :], in_=ident[:, :], compare_op=ALU.not_equal, fill=1.0,
                               base=0, pattern=[[-1, P]], channel_multiplier=1).then_inc(z_id, 1)
            pool.wait_ge(z_id, 1)
            pool.tensor_copy(ident_bf[:, :], ident[:, :]).then_inc(z_id, 1)
            pool.wait_ge(z_ms, 2)
            for n, g in enumerate(G3):
                if n:
                    pool.wait_ge(z_sel, n)
                pool.affine_select(out=rowsel[:, :, :], in_=rowsel[:, :, :], compare_op=ALU.not_equal, fill=1.0,
                                   base=-g, pattern=[[-1, 8], [0, P]], channel_multiplier=1).then_inc(z_sel, 1)
            pool.wait_ge(z_ms, 4)

            def rstd(name, p, mv, ve, rs):
                wait(pool, name + "_ag", p)
                pool.tensor_tensor(ve[p.e][:, :], mv[p.e][:, :, 1], eps[:, :], ALU.add).then_inc(S[name + "_ve"], 1)
                wait(pool, name + "_ve", p)
                pool.tensor_tensor(rs[p.e][:, :], ve[p.e][:, :], minus_half[:, :], ALU.pow).then_inc(S[name + "_rs"], 1)

            def h2_low(p, u):
                wait(pool, "h2_hi", p, u + 1)
                pool.tensor_tensor(h2_lo[:, u, :, :].rearrange("p c n -> p (c n)"), h2v[u % 2][:, :],
                                   h2_hi[:, u, :, :].rearrange("p c n -> p (c n)").bitcast(F32), ALU.subtract).then_inc(S["h2_lo"], 1)

            def soft(p, b):
                wait(pool, "z_r", p, b + 1)
                if b == 0:
                    wait(pool, "at_mm", p, lag=1)
                pool.tensor_tensor(zn[:, b, :, :], zp[:, b, :, :],
                                   zr[p.e][:, b, :].unsqueeze(2).broadcast_to([P, H, P]), ALU.mult).then_inc(S["z_n"], 1)

            def add_beta(p):
                if p.is_first():
                    pool.wait_ge(c_in, 80)
                pool.wait_ge(r_in[p.e], half(p))
                wait(pool, "x2", p, lag=2)
                pool.tensor_tensor(xb[p.e][:, :, :], xr[p.e][:, :, :],
                                   beta_bc[:, :].unsqueeze(1).broadcast_to([P, 2, F]), ALU.add).then_inc(S["xb"], 1)

            def add_bias(p):
                if p.is_first():
                    pool.wait_ge(set_dve, DVE_DEG)
                wait(pool, "x2", p)
                wait(pool, "o_sb", p, lag=1)
                pool.tensor_tensor(x2d[p.e][:, :, :], x2[p.e][:, :, :],
                                   deg_bias[:, :].unsqueeze(1).broadcast_to([P, 2, F]), ALU.add).then_inc(S["x2d"], 1)

            def rstd1(p):
                rstd("a", p, a_mv, a_ve, a_rs)

            def rstd2(p):
                rstd("b", p, b_mv, b_ve, b_rs)

            def rstd3(p):
                rstd("c", p, c_mv, c_ve, c_rs)

            def h_low(p):
                wait(pool, "h_hi", p)
                pool.tensor_tensor(h_lo[p.e][:, :, :], h[p.e][:, :, :], h_hi[p.e][:, :, :].bitcast(F32),
                                   ALU.subtract).then_inc(S["h_lo"], 1)

            def h3_low(p):
                wait(pool, "h3_hi", p)
                pool.tensor_tensor(h3_lo[:, :, :], h3[p.e][:, :, :], h3_hi[:, :, :].bitcast(F32),
                                   ALU.subtract).then_inc(S["h3_lo"], 1)

            def one(pairs):
                if p := pairs[3]:
                    h2_low(p, 3)
                if p := pairs[4]:
                    rstd2(p)
                if p := pairs[1]:
                    rstd1(p)
                if p := pairs[4]:
                    add_bias(p)
                    rstd3(p)
                if p := pairs[1]:
                    h_low(p)
                if p := pairs[2]:
                    h2_low(p, 0)
                if p := pairs[4]:
                    h3_low(p)
                if p := pairs[2]:
                    h2_low(p, 1)
                if p := pairs[3]:
                    add_beta(p)
                if p := pairs[1]:
                    soft(p, 0)
                    soft(p, 1)
                if p := pairs[2]:
                    h2_low(p, 2)
            def low_w_out():
                pool.wait_ge(set_act, ACT_WO)
                pool.tensor_tensor(wo_lo[:, :, :], wo[:, :, :], wo_hi[:, :, :].bitcast(F32), ALU.subtract).then_inc(set_pool, 1)

            steps(pool, one, [lambda: None, low_w_out])

        @block.vector
        def _(dve):
            own, chain = sem("dve_setup"), [0]

            def after(ins):
                chain[0] += 1
                ins.then_inc(own, 1)
                dve.wait_ge(own, chain[0])

            dots = [0]

            def dot(a, b, total):
                if dots[0] >= 4:
                    dve.wait_ge(dotted, dots[0] - 3)
                slot = res[dots[0] // 2 % 2][:, dots[0] % 2, :]
                dots[0] += 1
                dve.scalar_tensor_tensor(slot, a, 1.0, b, ALU.mult, ALU.mult, accum_out=total).then_inc(dotted, 1)

            dve.memset(wa_rep[:, :, :], 0.0).then_inc(set_dve, 1)
            dve.memset(f2_rep[0][:, :], 0.0).then_inc(set_dve, 1)
            dve.memset(f2_rep[1][:, :], 0.0).then_inc(set_dve, 1)
            dve.wait_ge(adj_in, 16)
            dve.tensor_copy(adj_f[:, :], adj_i[:, :]).then_inc(set_dve, 1)
            dve.wait_ge(set_dve, DVE_ADJ)
            dve.tensor_scalar(mask[:, :, :], adj_f[:, :].unsqueeze(1).broadcast_to([P, H, P]), 0.0, NEG,
                              ALU.is_le, ALU.mult).then_inc(set_dve, 1)

            def heads_weights():
                dve.wait_ge(heads_in, 48)
                for c in range(C):
                    for hd in range(H):
                        for j in range(2):
                            dot(wh[:, c, hd, :], ah_bc[:, hd, j * F:(j + 1) * F], wa[:, c, j, hd:hd + 1])
                dve.wait_ge(dotted, DOTS_HEADS)
                for c in range(C):
                    last = dve.tensor_copy(wa_rep[:, c, 32:P].rearrange("p (g r) -> p g r", r=32)[:, :, 0:2 * H],
                                           wa[:, c, :, :].rearrange("p j h -> p (j h)").unsqueeze(1).broadcast_to([P, 3, 2 * H]))
                last.then_inc(set_dve, 1)
                dve.wait_ge(set_act, ACT_WH)
                dve.tensor_tensor(wh_lo[:, :, :, :], wh[:, :, :, :], wh_hi[:, :, :, :].bitcast(F32), ALU.subtract)\
                   .then_inc(set_dve, 1)

            def later_weights():
                dve.wait_ge(out_in, 32)
                for k in range(K2):
                    for j in range(2):
                        dot(wo[:, k, 0:F], ao_bc[:, j, :], wo[:, k, F + j:F + j + 1])
                after(dve.reduce_sum(deg[:, :], adj_f[:, :], axis=X))
                dve.wait_ge(c_in, 80)
                dve.wait_ge(z_id, 2)
                dve.tensor_scalar(adj_deg[:, 1, :], ident[:, :], deg[:, 0:1], None, ALU.mult)
                dve.tensor_scalar(deg_bias[:, :], l1b_bc[:, :], deg[:, 0:1], None, ALU.mult).then_inc(set_dve, 1)
                after(dve.tensor_copy(b2_parts[:, :], b2_bc[:, :]))
                after(dve.tensor_tensor(b2_rest[64:P, :], b2_bc[64:P, :], b2_parts[64:P, :], ALU.subtract))
                after(dve.tensor_copy(b2_parts[64:P, :], b2_rest[64:P, :]))
                dve.tensor_tensor(b2_parts[96:P, :], b2_rest[96:P, :], b2_parts[96:P, :], ALU.subtract).then_inc(set_dve, 1)
                dve.wait_ge(set_pe, 1)
                dve.tensor_copy(adj_deg[:, 0, :], ps_z[:, 0, 0:P])
                dve.wait_ge(set_act, ACT_LAST)
                for s in range(2):
                    last = dve.tensor_tensor(l1w_lo[:, s, :, :].rearrange("p c o -> p (c o)"), ps_g[:, 2 + s, :],
                                             l1w_hi[:, s, :, :].rearrange("p c o -> p (c o)").bitcast(F32), ALU.subtract)
                last.then_inc(set_dve, 1)

            def stats(name, p, src, st):
                for b in range(2):
                    dve.bn_stats(st[p.e][:, b, :], src(b)).then_inc(S[name + "_bn"], 1)

            def mean_var(name, p, st, mv):
                for b in range(2):
                    wait(dve, name + "_bn", p, b + 1)
                    dve.nop(nofuse=True)
                    dve.bn_aggr(mv[p.e][:, b, :], st[p.e][:, b, :]).then_inc(S[name + "_ag"], 1)

            def shift(name, p, mv, rs, nm):
                wait(dve, name + "_rs", p)
                dve.scalar_tensor_tensor(nm[p.e][:, :], mv[p.e][:, :, 0], -1.0, rs[p.e][:, :], ALU.mult, ALU.mult)\
                   .then_inc(S[name + "_nm"], 1)

            def gh_low(p, u):
                b, c = u // 2, u % 2
                wait(dve, "gh_hi", p, u + 1)
                dve.tensor_tensor(gh_lo[:, c, :, b, :], ps_g[:, u % 2, :].rearrange("p (h n) -> p h n", h=H),
                                  gh_hi[:, c, :, b, :].bitcast(F32), ALU.subtract).then_inc(S["gh_lo"], 1)

            def less_first(name, p, psum, parts, rest):
                wait(dve, name + "_c", p)
                dve.tensor_tensor(rest[p.e][64:P, :], psum[64:P, :], parts[p.e][64:P, :], ALU.subtract)\
                   .then_inc(S[name + "_r"], 1)

            def second(name, p, parts, rest):
                wait(dve, name + "_r", p)
                dve.tensor_copy(parts[p.e][64:P, :], rest[p.e][64:P, :]).then_inc(S[name + "_m"], 1)

            def third(name, p, parts, rest):
                wait(dve, name + "_m", p)
                dve.tensor_tensor(parts[p.e][96:P, :], rest[p.e][96:P, :], parts[p.e][96:P, :], ALU.subtract)\
                   .then_inc(S[name + "_l"], 1)

            def f_less_first(p):
                less_first("f", p, ps_x[:, 0, 0:2 * P], f_parts, f_rest)

            def f_second(p):
                second("f", p, f_parts, f_rest)

            def f_third(p):
                third("f", p, f_parts, f_rest)

            def g_first(p):
                wait(dve, "fT_mm", p)
                wait(dve, "z2_mm", p, lag=2)
                dve.tensor_copy(g_parts[p.e][:, :], ps_z[:, 0, 0:P]).then_inc(S["fT_c"], 1)

            def g_less_first(p):
                less_first("fT", p, ps_z[:, 0, 0:P], g_parts, g_rest)

            def g_second(p):
                second("fT", p, g_parts, g_rest)

            def g_third(p):
                third("fT", p, g_parts, g_rest)

            def elu_min(p, u):
                i = u % 2
                wait(dve, "h2_e", p, u + 1)
                dve.tensor_scalar(h2e[i][:, :], h2e[i][:, :], 1.0, 0.0, ALU.subtract, ALU.min).then_inc(S["h2_u"], 1)

            def elu(p, u):
                i = u % 2
                wait(dve, "h2_u", p, u + 1)
                if u >= 2:
                    wait(dve, "h2_lo", p, u - 1)
                else:
                    wait(dve, "h2_lo", p, u + 3, lag=1)
                dve.tensor_tensor(h2v[i][:, :], h2e[i][:, :], ps_g[:, u % 2, :], ALU.max).then_inc(S["h2_v"], 1)

            def h2_high(p, u):
                wait(dve, "h2_v", p, u + 1)
                if u == 0:
                    wait(dve, "wh2_mm", p, lag=1)
                dve.tensor_copy(h2_hi[:, u, :, :].rearrange("p c n -> p (c n)"), h2v[u % 2][:, :]).then_inc(S["h2_hi"], 1)

            def soft_leaky(p, b):
                wait(dve, "z_t", p, b + 1)
                dve.scalar_tensor_tensor(zt[:, b, :, :], zt[:, b, :, :], 0.01, zt[:, b, :, :],
                                         ALU.mult, ALU.max).then_inc(S["z_d"], 1)

            def soft_max(p, b):
                wait(dve, "z_d", p, b + 1)
                dve.tensor_reduce(zm[p.e][:, b, :], zt[:, b, :, :], X, ALU.max, negate=True).then_inc(S["z_m"], 1)

            def soft_sum(p, b):
                wait(dve, "z_p", p, H * (b + 1))
                dve.reciprocal(zr[p.e][:, b, :], zs[p.e][:, b, :]).then_inc(S["z_r"], 1)

            def wh2_scores(p, b):
                wait(dve, "wh2_sb", p, b + 1)
                wait(dve, "fT_mm", p, lag=2)
                dve.tensor_copy(f2_rep[p.e][:, 32:P].rearrange("p (g r) -> p g r", r=32)[:, :, b:b + 3:2],
                                ps_g[:, 2 + b, F:WO].unsqueeze(1).broadcast_to([P, 3, 2])).then_inc(S["wh2_f"], 1)

            def soft_leaky2(p):
                wait(dve, "z2_t", p)
                dve.scalar_tensor_tensor(yt[p.e][:, :, :], yt[p.e][:, :, :], 0.01, yt[p.e][:, :, :],
                                         ALU.mult, ALU.max).then_inc(S["z2_d"], 1)

            def soft_max2(p):
                wait(dve, "z2_d", p)
                dve.tensor_reduce(ym[p.e][:, :], yt[p.e][:, :, :], X, ALU.max, negate=True).then_inc(S["z2_m"], 1)

            def soft_sum2(p):
                wait(dve, "z2_p", p)
                dve.reciprocal(yr[p.e][:, :], ys[p.e][:, :]).then_inc(S["z2_r"], 1)

            def soft2(p):
                wait(dve, "z2_r", p)
                wait(dve, "a2_mm", p, lag=1)
                dve.tensor_tensor(yn[p.e][:, :, :], yp[p.e][:, :, :],
                                  yr[p.e][:, :].unsqueeze(2).broadcast_to([P, 2, P]), ALU.mult).then_inc(S["z2_n"], 1)

            def out_min(p):
                wait(dve, "out_e", p)
                dve.tensor_scalar(oe[p.e][:, :, :], oe[p.e][:, :, :], 1.0, 0.0, ALU.subtract, ALU.min).then_inc(S["out_u"], 1)

            def out_elu(p):
                wait(dve, "out_u", p)
                wait(dve, "y_mm", p, lag=1)
                dve.tensor_tensor(ov[p.e][:, :, :], oe[p.e][:, :, :],
                                  ps_z[:, 1, :].rearrange("p (c n) -> p c n", c=C), ALU.max).then_inc(S["out_v"], 1)

            def norm2_stats(p):
                wait(dve, "y_mm", p)
                stats("b", p, lambda b: ps_z[:, 1, b * F:(b + 1) * F], b_st)

            def norm2_var(p):
                mean_var("b", p, b_st, b_mv)

            def norm2_shift(p):
                shift("b", p, b_mv, b_rs, b_nm)

            def scale2(p):
                wait(dve, "lt", p)
                dve.tensor_tensor(lt[p.e][:, :, :], lt[p.e][:, :, :],
                                  gamma_bc[:, :].unsqueeze(1).broadcast_to([P, 2, F]), ALU.mult).then_inc(S["lg"], 1)

            def residual2(p):
                wait(dve, "lg", p)
                wait(dve, "xb", p)
                wait(dve, "h3", p, lag=1)
                wait(dve, "x2d", p, lag=1)
                dve.tensor_tensor(x2[p.e][:, :, :], lt[p.e][:, :, :], xb[p.e][:, :, :], ALU.add).then_inc(S["x2"], 1)

            def norm3_stats(p):
                wait(dve, "x2", p)
                stats("c", p, lambda b: x2[p.e][:, b, :], c_st)

            def norm3_var(p):
                mean_var("c", p, c_st, c_mv)

            def norm3_shift(p):
                shift("c", p, c_mv, c_rs, c_nm)

            def h3_high(p):
                wait(dve, "h3", p)
                wait(dve, "gd_mm", p, lag=1)
                dve.tensor_copy(h3_hi[:, :, :], h3[p.e][:, :, :]).then_inc(S["h3_hi"], 1)

            def at_low(p, b):
                wait(dve, "at_hi", p, b + 1)
                dve.tensor_tensor(at_lo[p.e][:, b, :], ps_x[:, b, :], at_hi[p.e][:, b, :].bitcast(F32),
                                  ALU.subtract).then_inc(S["at_lo"], 1)

            def norm1_stats(p):
                dve.wait_ge(x_in[p.e], half(p))
                stats("a", p, lambda b: xa[p.e][:, b, :], a_st)

            def norm1_var(p):
                mean_var("a", p, a_st, a_mv)

            def norm1_shift(p):
                shift("a", p, a_mv, a_rs, a_nm)

            def h_high(p):
                wait(dve, "h_sb", p)
                wait(dve, "gh_mm", p, lag=2)
                dve.tensor_copy(h_hi[p.e][:, :, :], h[p.e][:, :, :]).then_inc(S["h_hi"], 1)

            def gd_low(p, b):
                wait(dve, "gd_hi", p, b + 1)
                dve.tensor_tensor(gd_lo[:, b, :, :, :], ps_x[:, b, :].rearrange("p (c s n) -> p c s n", c=C, s=2),
                                  gd_hi[:, b, :, :, :].bitcast(F32), ALU.subtract).then_inc(S["gd_lo"], 1)

            def result(p):
                wait(dve, "o_mm", p)
                wait(dve, "x2d", p)
                if p.lagged(2).exists():
                    dve.wait_ge(stored[p.e], half(p, 2))
                dve.tensor_tensor(res[p.e][:, :, :], x2d[p.e][:, :, :],
                                  ps_x[:, 0, :].rearrange("p (b o) -> p b o", b=2), ALU.add).then_inc(S["o_sb"], 1)

            def one(pairs):
                if p := pairs[2]:
                    at_low(p, 0)
                if p := pairs[4]:
                    norm2_stats(p)
                if p := pairs[2]:
                    at_low(p, 1)
                if p := pairs[4]:
                    norm2_var(p)
                if p := pairs[1]:
                    norm1_stats(p)
                    norm1_var(p)
                if p := pairs[4]:
                    norm2_shift(p)
                if p := pairs[2]:
                    gh_low(p, 0)
                if p := pairs[5]:
                    result(p)
                if p := pairs[4]:
                    scale2(p)
                    residual2(p)
                if p := pairs[1]:
                    norm1_shift(p)
                if p := pairs[3]:
                    wh2_scores(p, 0)
                if p := pairs[2]:
                    gh_low(p, 1)
                if p := pairs[4]:
                    norm3_stats(p)
                    norm3_var(p)
                if p := pairs[1]:
                    h_high(p)
                if p := pairs[2]:
                    gh_low(p, 2)
                if p := pairs[4]:
                    norm3_shift(p)
                if p := pairs[3]:
                    wh2_scores(p, 1)
                if p := pairs[2]:
                    gh_low(p, 3)
                if p := pairs[3]:
                    g_first(p)
                    g_less_first(p)
                    g_second(p)
                    g_third(p)
                    soft_leaky2(p)
                if p := pairs[2]:
                    elu_min(p, 0)
                if p := pairs[3]:
                    soft_max2(p)
                if p := pairs[2]:
                    elu(p, 0)
                    h2_high(p, 0)
                if p := pairs[3]:
                    soft_sum2(p)
                    soft2(p)
                if p := pairs[1]:
                    f_less_first(p)
                    f_second(p)
                    f_third(p)
                if p := pairs[4]:
                    h3_high(p)
                if p := pairs[2]:
                    elu_min(p, 1)
                    elu(p, 1)
                    h2_high(p, 1)
                if p := pairs[1]:
                    soft_leaky(p, 0)
                    soft_max(p, 0)
                if p := pairs[3]:
                    out_min(p)
                    out_elu(p)
                if p := pairs[1]:
                    soft_leaky(p, 1)
                    soft_max(p, 1)
                    soft_sum(p, 0)
                if p := pairs[2]:
                    elu_min(p, 2)
                    elu(p, 2)
                if p := pairs[1]:
                    soft_sum(p, 1)
                if p := pairs[2]:
                    h2_high(p, 2)
                if p := pairs[4]:
                    gd_low(p, 0)
                    gd_low(p, 1)
                if p := pairs[2]:
                    elu_min(p, 3)
                    elu(p, 3)
                    h2_high(p, 3)
            steps(dve, one, [heads_weights, later_weights])

        @block.scalar
        def _(act):
            def heads_weights():
                act.wait_ge(heads_in, 48)
                act.activation(wh_hi[:, :, :, :], wh[:, :, :, :], ACT.Copy).then_inc(set_act, 1)

            def later_weights():
                act.wait_ge(dotted, DOTS_ALL)
                act.activation(wo_hi[:, :, :], wo[:, :, :], ACT.Copy).then_inc(set_act, 1)
                act.wait_ge(set_pe, 1)
                for s in range(2):
                    act.activation(l1w_hi[:, s, :, :].rearrange("p c o -> p (c o)"), ps_g[:, 2 + s, :], ACT.Copy)\
                       .then_inc(set_act, 1)

            def gh_high(p, u):
                b, c = u // 2, u % 2
                wait(act, "gh_mm", p, u + 1)
                if u == 0:
                    wait(act, "h2_mm", p, lag=1)
                act.activation(gh_hi[:, c, :, b, :], ps_g[:, u % 2, :].rearrange("p (h n) -> p h n", h=H),
                               ACT.Copy).then_inc(S["gh_hi"], 1)

            def elu_exp(p, u):
                if p.is_first() and u == 0:
                    act.wait_ge(set_pool, POOL_WO)
                if u >= 2:
                    wait(act, "h2_v", p, u - 1)
                else:
                    wait(act, "h2_v", p, u + 3, lag=1)
                wait(act, "h2_mm", p, u + 1)
                act.activation(h2e[u % 2][:, :], ps_g[:, u % 2, :], ACT.Exp).then_inc(S["h2_e"], 1)

            def score_copy(p, b):
                wait(act, "z_mm", p, b + 1)
                act.activation(zt[:, b, :, :], ps_x[:, b, :].rearrange("p (h m) -> p h m", h=H), ACT.Copy)\
                   .then_inc(S["z_t"], 1)

            def soft_exp(p, b):
                wait(act, "z_d", p, b + 1)
                wait(act, "z_m", p, b + 1)
                if b == 0:
                    wait(act, "z_n", p, lag=1)
                for hd in range(H):
                    act.activation(zp[:, b, hd, :], zt[:, b, hd, :], ACT.Exp, bias=zm[p.e][:, b, hd:hd + 1],
                                   accum_out=zs[p.e][:, b, hd:hd + 1]).then_inc(S["z_p"], 1)

            def wh2_copy(p, b):
                wait(act, "wh2_mm", p, b + 1)
                wait(act, "out_mm", p, lag=1)
                act.activation(wh2[p.e][:, b, :], ps_g[:, 2 + b, 0:F], ACT.Copy).then_inc(S["wh2_sb"], 1)

            def normal(name, p, dst, src, rs, nm, func, done):
                wait(act, name + "_nm", p)
                for b in range(2):
                    act.activation(dst[p.e][:, b, :], src(b), func, bias=nm[p.e][:, b:b + 1],
                                   scale=rs[p.e][:, b:b + 1]).then_inc(S[done], 1)

            def ht_copy(p):
                wait(act, "ht_mm", p)
                wait(act, "f_mm", p, lag=1)
                act.activation(ht[p.e][:, :, :], ps_x[:, 1, :].rearrange("p (c n) -> p c n", c=C), ACT.Copy)\
                   .then_inc(S["ht_sb"], 1)

            def f_copy(p):
                wait(act, "f_mm", p)
                wait(act, "z_mm", p, lag=1)
                act.activation(f_parts[p.e][:, :], ps_x[:, 0, 0:2 * P], ACT.Copy).then_inc(S["f_c"], 1)

            def score_copy2(p):
                wait(act, "z2_mm", p)
                act.activation(yt[p.e][:, :, :], ps_z[:, 1, 0:2 * P].rearrange("p (b m) -> p b m", b=2), ACT.Copy)\
                   .then_inc(S["z2_t"], 1)

            def soft_exp2(p):
                wait(act, "z2_m", p)
                for b in range(2):
                    act.activation(yp[p.e][:, b, :], yt[p.e][:, b, :], ACT.Exp, bias=ym[p.e][:, b:b + 1],
                                   accum_out=ys[p.e][:, b:b + 1]).then_inc(S["z2_p"], 1)

            def a2_copy(p):
                wait(act, "a2_mm", p)
                wait(act, "out_mm", p, lag=1)
                act.activation(a2t[p.e][:, :, :], ps_z[:, 0, 0:2 * P].rearrange("p (b m) -> p b m", b=2), ACT.Copy)\
                   .then_inc(S["a2_sb"], 1)

            def out_exp(p):
                wait(act, "out_mm", p)
                wait(act, "out_v", p, lag=1)
                act.activation(oe[p.e][:, :, :], ps_z[:, 1, :].rearrange("p (c n) -> p c n", c=C), ACT.Exp)\
                   .then_inc(S["out_e"], 1)

            def hidden_relu(p):
                if p.is_first():
                    act.wait_ge(c_in, 80)
                wait(act, "hid_mm", p)
                wait(act, "y_mm", p, lag=1)
                for c in range(C):
                    act.activation(hid[p.e][:, c, :], ps_z[:, 0, c * 2 * P:(c + 1) * 2 * P], ACT.Relu,
                                   bias=b1_col[:, c:c + 1]).then_inc(S["hid_sb"], 1)

            def norm2(p):
                wait(act, "x2", p, lag=1)
                normal("b", p, lt, lambda b: ps_z[:, 1, b * F:(b + 1) * F], b_rs, b_nm, ACT.Identity, "lt")

            def norm3(p):
                wait(act, "h3_lo", p, lag=1)
                normal("c", p, h3, lambda b: x2[p.e][:, b, :], c_rs, c_nm, ACT.Relu, "h3")

            def norm1(p):
                wait(act, "h_lo", p, lag=2)
                wait(act, "ht_mm", p, lag=2)
                normal("a", p, h, lambda b: xa[p.e][:, b, :], a_rs, a_nm, ACT.Relu, "h_sb")

            def at_high(p, b):
                wait(act, "at_mm", p, b + 1)
                wait(act, "gh_mm", p, lag=2)
                act.activation(at_hi[p.e][:, b, :], ps_x[:, b, :], ACT.Copy).then_inc(S["at_hi"], 1)

            def gd_high(p, b):
                wait(act, "gd_mm", p, b + 1)
                wait(act, "o_mm", p, lag=1)
                act.activation(gd_hi[:, b, :, :, :], ps_x[:, b, :].rearrange("p (c s n) -> p c s n", c=C, s=2),
                               ACT.Copy).then_inc(S["gd_hi"], 1)

            def one(pairs):
                if p := pairs[2]:
                    at_high(p, 0)
                    at_high(p, 1)
                    gh_high(p, 0)
                if p := pairs[4]:
                    norm2(p)
                if p := pairs[3]:
                    wh2_copy(p, 0)
                if p := pairs[2]:
                    gh_high(p, 1)
                if p := pairs[1]:
                    norm1(p)
                if p := pairs[2]:
                    gh_high(p, 2)
                if p := pairs[3]:
                    wh2_copy(p, 1)
                if p := pairs[2]:
                    gh_high(p, 3)
                if p := pairs[3]:
                    score_copy2(p)
                if p := pairs[2]:
                    elu_exp(p, 0)
                if p := pairs[1]:
                    ht_copy(p)
                if p := pairs[3]:
                    soft_exp2(p)
                if p := pairs[1]:
                    f_copy(p)
                if p := pairs[4]:
                    norm3(p)
                if p := pairs[2]:
                    elu_exp(p, 1)
                if p := pairs[3]:
                    a2_copy(p)
                if p := pairs[1]:
                    score_copy(p, 0)
                    score_copy(p, 1)
                if p := pairs[3]:
                    out_exp(p)
                if p := pairs[1]:
                    soft_exp(p, 0)
                if p := pairs[2]:
                    elu_exp(p, 2)
                if p := pairs[1]:
                    soft_exp(p, 1)
                if p := pairs[3]:
                    hidden_relu(p)
                if p := pairs[4]:
                    gd_high(p, 0)
                    gd_high(p, 1)
                if p := pairs[2]:
                    elu_exp(p, 3)
            steps(act, one, [heads_weights, later_weights])

        @block.tensor
        def _(pe):
            pe.wait_ge(z_id, 2)

            def later_weights():
                pe.wait_ge(last_in, 16)
                pe.wait_ge(set_dve, DVE_ADJ)
                pe.transpose(ps_z[:, 0, 0:P], adj_f[:, :], ident[:, :])
                for s in range(2):
                    for c in range(C):
                        for k in range(C):
                            last = pe.transpose(ps_g[:, 2 + s, c * F + k * P:c * F + (k + 1) * P],
                                                l1w_sb[:, k, s * F + c * P:s * F + (c + 1) * P], ident[:, :])
                last.then_inc(set_pe, 1)

            def mm(out_, lhs, rhs, start, stop):
                return pe.matmul(out_, lhs, rhs, start=start, stop=stop)

            def three(out_, lhs, rhs, first, last):
                mm(out_, lhs[0], rhs[0], first, False)
                mm(out_, lhs[0], rhs[1], False, False)
                return mm(out_, lhs[1], rhs[0], False, last)

            def gh_unit(p, u):
                b, c = u // 2, u % 2
                if u == 0:
                    wait(pe, "h_lo", p)
                wait(pe, "at_lo", p, b + 1)
                if u == 0:
                    wait(pe, "h2_v", p, 3, lag=1)
                if u == 1:
                    wait(pe, "h2_v", p, 4, lag=1)
                if u == 2:
                    wait(pe, "gh_lo", p, 1)
                if u == 3:
                    wait(pe, "gh_lo", p, 2)
                cols = slice(c * P, (c + 1) * P)
                three(ps_g[:, u % 2, :], (h_hi[p.e][:, b, cols], h_lo[p.e][:, b, cols]),
                      (at_hi[p.e][:, b, :], at_lo[p.e][:, b, :]), True, True).then_inc(S["gh_mm"], 1)

            def h2_unit(p, u):
                if p.is_first() and u == 0:
                    pe.wait_ge(set_dve, DVE_WH)
                if u == 0:
                    wait(pe, "gh_lo", p)
                if u == 2:
                    wait(pe, "h2_v", p, 1)
                if u == 3:
                    wait(pe, "h2_v", p, 2)
                for oc in range(C):
                    for c in range(C):
                        cols = slice(oc * P, (oc + 1) * P)
                        last = three(ps_g[:, u % 2, oc * 2 * P:(oc + 1) * 2 * P],
                                     (wh_hi[:, c, u, cols], wh_lo[:, c, u, cols]),
                                     (gh_hi[:, c, u, :, :].rearrange("p b n -> p (b n)"),
                                      gh_lo[:, c, u, :, :].rearrange("p b n -> p (b n)")), c == 0, c == C - 1)
                last.then_inc(S["h2_mm"], 1)

            def wh2_part(p, b, k0, k1):
                if p.is_first() and b == k0 == 0:
                    pe.wait_ge(set_pool, POOL_WO)
                    pe.wait_ge(set_dve, DVE_LAST)
                if k0 == 0:
                    wait(pe, "wh2_f", p, b + 1, lag=1)
                rows = slice(b * P, (b + 1) * P)
                for k in range(k0, k1):
                    if b == 0 and k % C == 0:
                        wait(pe, "h2_lo", p, k // C + 1)
                    last = three(ps_g[:, 2 + b, 0:WO], (h2_hi[:, k // C, k % C, rows], h2_lo[:, k // C, k % C, rows]),
                                 (wo_hi[:, k, :], wo_lo[:, k, :]), k == 0, k == K2 - 1)
                if k1 == K2:
                    last.then_inc(S["wh2_mm"], 1)

            def h_transposes(p):
                wait(pe, "h_sb", p)
                wait(pe, "at_lo", p, 2, lag=1)
                for c in range(C):
                    for b in range(2):
                        last = pe.transpose(ps_x[:, 1, (c * 2 + b) * P:(c * 2 + b + 1) * P],
                                            h[p.e][:, b, c * P:(c + 1) * P], ident[:, :])
                last.then_inc(S["ht_mm"], 1)

            def score_rows(p):
                if p.is_first():
                    pe.wait_ge(set_dve, DVE_WA)
                wait(pe, "ht_sb", p)
                wait(pe, "o_sb", p, 1, lag=4)
                for c in range(C):
                    last = mm(ps_x[:, 0, 0:2 * P], wa_rep[:, c, :], ht[p.e][:, c, :], c == 0, c == C - 1)
                last.then_inc(S["f_mm"], 1)

            def scores(p):
                if p.is_first():
                    pe.wait_ge(z_sel, 3)
                wait(pe, "f_l", p)
                for b in range(2):
                    rows = f_parts[p.e][:, b * P:(b + 1) * P]
                    mm(ps_x[:, b, :], ident_bf[:, :], mask[:, :, :].rearrange("p h m -> p (h m)"), True, False)
                    mm(ps_x[:, b, :], rows, rowsel[:, 0:H, :].rearrange("p h m -> p (h m)"), False, False)
                    for hd in range(H):
                        last = mm(ps_x[:, b, hd * P:(hd + 1) * P], rowsel[:, H + hd, :], rows, False, hd == H - 1)
                    last.then_inc(S["z_mm"], 1)

            def prob_transposes(p, b):
                wait(pe, "z_n", p, b + 1)
                if b == 0:
                    wait(pe, "gd_lo", p, 1, lag=3)
                if b == 1:
                    wait(pe, "gd_lo", p, 2, lag=3)
                for hd in range(H):
                    last = pe.transpose(ps_x[:, b, hd * P:(hd + 1) * P], zn[:, b, hd, :], ident[:, :])
                last.then_inc(S["at_mm"], 1)

            def score_rows2(p):
                wait(pe, "wh2_f", p)
                wait(pe, "hid_sb", p, 2, lag=1)
                pe.transpose(ps_z[:, 0, 0:P], f2_rep[p.e][:, :], ident[:, :]).then_inc(S["fT_mm"], 1)

            def scores2(p):
                wait(pe, "fT_l", p)
                wait(pe, "lt", p, 2, lag=1)
                mm(ps_z[:, 1, 0:2 * P], ident_bf[:, :], mask[:, 0:2, :].rearrange("p b m -> p (b m)"), True, False)
                mm(ps_z[:, 1, 0:2 * P], g_parts[p.e][:, :], rowsel[:, 0:2, :].rearrange("p b m -> p (b m)"), False, False)
                for b in range(2):
                    last = mm(ps_z[:, 1, b * P:(b + 1) * P], rowsel[:, 2 + b, :], g_parts[p.e][:, :], False, b == 1)
                last.then_inc(S["z2_mm"], 1)

            def prob_transposes2(p):
                wait(pe, "z2_n", p)
                for b in range(2):
                    last = pe.transpose(ps_z[:, 0, b * P:(b + 1) * P], yn[p.e][:, b, :], ident[:, :])
                last.then_inc(S["a2_mm"], 1)

            def out2(p):
                wait(pe, "a2_sb", p)
                wait(pe, "wh2_sb", p)
                for oc in range(C):
                    for b in range(2):
                        last = mm(ps_z[:, 1, (oc * 2 + b) * P:(oc * 2 + b + 1) * P],
                                  wh2[p.e][:, b, oc * P:(oc + 1) * P], a2t[p.e][:, b, :], True, True)
                last.then_inc(S["out_mm"], 1)

            def hidden(p):
                if p.is_first():
                    pe.wait_ge(ffn_in, 32)
                wait(pe, "out_v", p)
                for dc in range(C):
                    for c in range(C):
                        last = mm(ps_z[:, 0, dc * 2 * P:(dc + 1) * 2 * P], w1_sb[:, c, dc * P:(dc + 1) * P],
                                  ov[p.e][:, c, :], c == 0, c == C - 1)
                    last.then_inc(S["hid_mm"], 1)

            def ffn(p, b):
                wait(pe, "hid_sb", p)
                rows = slice(b * P, (b + 1) * P)
                mm(ps_z[:, 1, b * F:(b + 1) * F], rowsel[:, 0, :], b2_parts[:, :], True, False)
                for c in range(C):
                    mm(ps_z[:, 1, b * F + c * P:b * F + (c + 1) * P], ov[p.e][:, c, rows], ident[:, :], False, False)
                for c in range(C):
                    last = mm(ps_z[:, 1, b * F:(b + 1) * F], hid[p.e][:, c, rows], w2_sb[:, c, :], False, c == C - 1)
                last.then_inc(S["y_mm"], 1)

            def gather(p, b):
                wait(pe, "h3_lo", p)
                if b == 0:
                    wait(pe, "z_t", p, 1, lag=-3)
                if b == 1:
                    wait(pe, "z_t", p, 2, lag=-3)
                right = adj_deg[:, :, :].rearrange("p s n -> p (s n)")
                for c in range(C):
                    cols = slice(c * P, (c + 1) * P)
                    mm(ps_x[:, b, c * F:(c + 1) * F], h3_hi[:, b, cols], right, True, False)
                    last = mm(ps_x[:, b, c * F:(c + 1) * F], h3_lo[:, b, cols], right, False, True)
                last.then_inc(S["gd_mm"], 1)

            def last_product(p, b):
                if b == 0:
                    wait(pe, "gd_lo", p)
                if b == 0:
                    wait(pe, "at_lo", p, 1, lag=-3)
                for s in range(2):
                    for c in range(C):
                        last = three(ps_x[:, 0, b * F:(b + 1) * F], (gd_hi[:, b, c, s, :], gd_lo[:, b, c, s, :]),
                                     (l1w_hi[:, 1 - s, c, :], l1w_lo[:, 1 - s, c, :]),
                                     s == 0 and c == 0, s == 1 and c == C - 1)
                if b == 1:
                    last.then_inc(S["o_mm"], 1)

            def one(pairs):
                if p := pairs[4]:
                    ffn(p, 1)
                if p := pairs[2]:
                    prob_transposes(p, 1)
                if p := pairs[3]:
                    wh2_part(p, 0, 0, 4)
                if p := pairs[5]:
                    last_product(p, 0)
                if p := pairs[2]:
                    gh_unit(p, 0)
                if p := pairs[5]:
                    last_product(p, 1)
                if p := pairs[3]:
                    wh2_part(p, 0, 4, 8)
                if p := pairs[2]:
                    gh_unit(p, 1)
                    gh_unit(p, 2)
                if p := pairs[3]:
                    wh2_part(p, 1, 0, 4)
                    wh2_part(p, 1, 4, 8)
                if p := pairs[2]:
                    gh_unit(p, 3)
                if p := pairs[3]:
                    score_rows2(p)
                if p := pairs[2]:
                    h2_unit(p, 0)
                if p := pairs[3]:
                    scores2(p)
                if p := pairs[1]:
                    h_transposes(p)
                    score_rows(p)
                if p := pairs[2]:
                    h2_unit(p, 1)
                if p := pairs[3]:
                    prob_transposes2(p)
                if p := pairs[1]:
                    scores(p)
                if p := pairs[3]:
                    out2(p)
                if p := pairs[4]:
                    gather(p, 0)
                if p := pairs[2]:
                    h2_unit(p, 2)
                if p := pairs[3]:
                    hidden(p)
                if p := pairs[2]:
                    h2_unit(p, 3)
                if p := pairs[4]:
                    gather(p, 1)
                if p := pairs[3]:
                    ffn(p, 0)
                if p := pairs[1]:
                    prob_transposes(p, 0)
            steps(pe, one, [lambda: None, later_weights])


NAMES = ["x", "adj", "L0_gnn_W_heads", "L0_gnn_a_heads", "L0_gnn_W_out", "L0_gnn_a_out", "L0_gnn_w1", "L0_gnn_b1",
         "L0_gnn_w2", "L0_gnn_b2", "L0_gnn_ln_gamma", "L0_gnn_ln_beta", "L1_gnn_W", "L1_gnn_b"]


def kernel(**inputs):
    import concourse.bacc as bacc
    from concourse.bass_utils import run_bass_kernel_spmd

    nc = bacc.Bacc("TRN2", target_bir_lowering=False, num_devices=1)
    arrays, args = {}, []
    for name in NAMES:
        a = np.ascontiguousarray(inputs[name])
        arrays[f"in_{name}"] = a
        args.append(nc.dram_tensor(f"in_{name}", a.shape, mybir.dt.from_np(a.dtype), kind="ExternalInput").ap())
    args.append(nc.dram_tensor("out_0", (BATCH, P, F), F32, kind="ExternalOutput").ap())
    build(nc, *args)
    r = run_bass_kernel_spmd(nc, [arrays], core_ids=[0])
    return r.results[0]["out_0"]
```

```python
import numpy as np
from contextlib import ExitStack

import concourse.bass as bass
from concourse import mybir

F32 = mybir.dt.float32
F32R = mybir.dt.float32r
BF16 = mybir.dt.bfloat16
I32 = mybir.dt.int32
ALU = mybir.AluOpType
ACT = mybir.ActivationFunctionType
X = mybir.AxisListType.X

P = 128
BATCH = 64
F = 256
C = F // P
H = 4
K2 = H * C
PAIRS = BATCH // 2
NEG = -1.0e30
EPS = 1e-5
G3 = (32, 64, 96)
TURNS = 4
STAGES = 6
WO = F + 2


class Pair:

    def __init__(self, i, c):
        self.i, self.c, self.e = i + c // 2, c % 2, c % 2

    def lagged(self, lag):
        return Pair(self.i, self.c - lag)

    def exists(self):
        return not isinstance(self.i, int) or 0 <= 2 * self.i + self.c < PAIRS

    def is_first(self):
        return isinstance(self.i, int) and 2 * self.i + self.c == 0

    def count(self, per, k):
        if isinstance(self.i, int):
            return per * (2 * self.i + self.c) + k
        return self.i * (2 * per) + (self.c * per + k)


def build(nc, x, adj, w_heads, a_heads, w_out, a_out, w1, b1, w2, b2, gamma, beta, l1w, l1b, out):
    ctx = ExitStack()
    with ctx:
        def sb(name, shape, dt=F32):
            return ctx.enter_context(nc.sbuf_tensor(name, shape, dt))

        def sem(name):
            return ctx.enter_context(nc.semaphore(name))

        def two(name, shape, dt=F32):
            return [sb(f"{name}{e}", shape, dt) for e in range(2)]

        def same(name, shape, dt=F32):
            return [sb(name, shape, dt)] * 2

        ident = sb("ident", [P, P])
        ident_bf = sb("ident_bf", [P, P], BF16)
        rowsel = sb("rowsel", [P, 4 * H, P], BF16)
        adj_i = sb("adj_i", [P, P], I32)
        adj_f = sb("adj_f", [P, P])
        mask = sb("mask", [P, P])
        mask_bf = sb("mask_bf", [P, 2, P], BF16)
        deg = sb("deg", [P, 1])
        adj_deg = sb("adj_deg", [P, 2, P], F32R)
        lend = sb("lend", [P, 4, 2 * F])
        wh = lend[:, :, :].rearrange("p (c g) (s o) -> p c (g s) o", c=C, s=2)
        lt, x2, x2d, h3 = ([lend[:, k, :].rearrange("p (b o) -> p b o", b=2)] * 2 for k in range(4))
        wh_hi = sb("wh_hi", [P, C, H, F], F32R)
        wh_lo = sb("wh_lo", [P, C, H, F], F32R)
        h2e, h2v = (two(n, [P, C * 2 * P]) for n in ("h2e", "h2v"))
        wo = sb("wo", [P, K2, F])
        wo_a = sb("wo_a", [P, K2, 2])
        wo_hi = sb("wo_hi", [P, K2, WO], F32R)
        wo_lo = sb("wo_lo", [P, K2, WO], F32R)
        lend2 = sb("lend2", [P, 3, 2, H, P])
        ah_bc = lend2[:, 0:2, :, :, :].rearrange("p x y h m -> p (x y) (h m)")
        zt, zp, zn = (lend2[:, k, :, :, :] for k in range(3))
        ao_bc = sb("ao_bc", [P, 2, F])
        wa = sb("wa", [P, C, 2, H])
        w1_sb = sb("w1_sb", [P, C, F])
        w2_sb = sb("w2_sb", [P, C, F])
        b1_col = sb("b1_col", [P, C])
        b2_col = sb("b2_col", [P, C])
        gamma_bc = sb("gamma_bc", [P, F])
        beta_bc = sb("beta_bc", [P, F])
        l1b_bc = sb("l1b_bc", [P, F])
        deg_bias = sb("deg_bias", [P, F])
        l1w_sb = sb("l1w_sb", [P, C, 2 * F])
        l1w_hi = sb("l1w_hi", [P, 2, C, F], F32R)
        l1w_lo = sb("l1w_lo", [P, 2, C, F], F32R)
        minus_half = sb("minus_half", [P, 2])
        eps = sb("eps", [P, 2])

        xa = two("xa", [P, 2, F])
        xr = two("xr", [P, 2, F])
        a_st, a_mv, a_ve, a_rs, a_nm = (two(n, s) for n, s in (
            ("a_st", [P, 2, 6]), ("a_mv", [P, 2, 2]), ("a_ve", [P, 2]), ("a_rs", [P, 2]), ("a_nm", [P, 2])))
        h = two("h", [P, 2, F])
        h_hi = two("h_hi", [P, 2, F], F32R)
        h_lo = two("h_lo", [P, 2, F], F32R)
        ht = same("ht", [P, C, 2 * P])
        f_rep = same("f_rep", [P, P])
        f_parts = same("f_parts", [P, P], BF16)
        f_rest = same("f_rest", [P, P])
        zm, zs, zr = (two(n, [P, 2, H]) for n in ("zm", "zs", "zr"))
        at_hi = two("at_hi", [P, 2, H * P], F32R)
        at_lo = two("at_lo", [P, 2, H * P], F32R)
        gh_hi = sb("gh_hi", [P, C, H, 2, P], F32R)
        gh_lo = sb("gh_lo", [P, C, H, 2, P], F32R)
        h2_hi = sb("h2_hi", [P, H, C, 2 * P], F32R)
        h2_lo = sb("h2_lo", [P, H, C, 2 * P], F32R)
        wh2 = same("wh2", [P, 2, F])
        f2_rep = two("f2_rep", [P, P])
        g_parts = two("g_parts", [P, P], BF16)
        g_rest = two("g_rest", [P, P])
        ym, ys, yr = (two(n, [P, 2]) for n in ("ym", "ys", "yr"))
        yt, yp, yn = (same(n, [P, 2, P]) for n in ("yt", "yp", "yn"))
        a2t = two("a2t", [P, 2, P])
        oe, ov = (same(n, [P, C, 2 * P]) for n in ("oe", "ov"))
        hid = same("hid", [P, C, 2 * P])
        b_st, b_mv, b_ve, b_rs, b_nm = (two(n, s) for n, s in (
            ("b_st", [P, 2, 6]), ("b_mv", [P, 2, 2]), ("b_ve", [P, 2]), ("b_rs", [P, 2]), ("b_nm", [P, 2])))
        c_st, c_mv, c_ve, c_rs, c_nm = (two(n, s) for n, s in (
            ("c_st", [P, 2, 6]), ("c_mv", [P, 2, 2]), ("c_ve", [P, 2]), ("c_rs", [P, 2]), ("c_nm", [P, 2])))
        xb = same("xb", [P, 2, F])
        h3_hi = sb("h3_hi", [P, 2, F], F32R)
        h3_lo = sb("h3_lo", [P, 2, F], F32R)
        gd_hi = sb("gd_hi", [P, 2, C, 2, P], F32R)
        gd_lo = sb("gd_lo", [P, 2, C, 2, P], F32R)
        res = two("res", [P, 2, F])

        ps_g = ctx.enter_context(nc.psum_tensor("ps_g", [P, 4, 512], F32))
        ps_x = ctx.enter_context(nc.psum_tensor("ps_x", [P, 2, 512], F32))
        ps_z = ctx.enter_context(nc.psum_tensor("ps_z", [P, 2, 512], F32))

        heads_in, out_in, ffn_in, last_in = sem("heads_in"), sem("out_in"), sem("ffn_in"), sem("last_in")
        adj_in, consts_in, memset_done, ident_ready, rowsel_ready = sem("adj_in"), sem("consts_in"), sem("memset_done"), sem("ident_ready"), sem("rowsel_ready")
        dve_setup, pe_setup, act_setup, pool_setup = sem("dve_setup"), sem("pe_setup"), sem("act_setup"), sem("pool_setup")
        dotted = sem("dotted")
        x_in = [sem(f"x_in{e}") for e in range(2)]
        r_in = [sem(f"r_in{e}") for e in range(2)]
        stored = [sem(f"stored{e}") for e in range(2)]
        S, PER = {}, {}
        for per, names in (
            (2, "x_stats x_moments h_ready"),
            (1, "x_variance x_rstd x_shift h_hi h_lo"),
            (1, "ht_done ht_copied cols_done cols_copied rows_done rows_first rows_rest rows_second "
                "rows_third"),
            (2, "scores_done scores_copied scores_leaky scores_masked scores_max sums_inverted "
                "probs_ready probs_transposed at_hi at_lo"),
            (2 * H, "exps_done"),
            (4, "gh_done gh_hi gh_lo heads_done heads_exp heads_min heads_elu heads_hi heads_lo"),
            (2, "wh2_done wh2_copied wh2_scores_copied exps2_done"),
            (1, "rows2_done rows2_first rows2_rest rows2_second rows2_third scores2_done "
                "scores2_copied scores2_leaky scores2_max sums2_inverted probs2_ready "
                "probs2_transposed probs2_copied"),
            (1, "out_done out_exp out_min out_elu ffn_done"),
            (2, "hidden_done hidden_ready ffn_plus_out ffn_transposed"),
            (2, "ffn_stats ffn_moments normal2_ready"),
            (1, "ffn_variance ffn_rstd ffn_shift normal2_scaled x_plus_beta x2_ready"),
            (2, "x2_stats x2_moments h3_ready"),
            (1, "x2_variance x2_rstd x2_shift h3_hi h3_lo"),
            (2, "gather_done gd_hi gd_lo"),
            (1, "last_done x2_plus_bias result_ready")):
            for n in names.split():
                S[n], PER[n] = sem(n), per

        def wait(eng, name, p, k=None, lag=0):
            q = p.lagged(lag)
            if q.exists():
                eng.wait_ge(S[name], q.count(PER[name], PER[name] if k is None else k))

        def half(p, lag=0):
            return (p.lagged(lag).i + 1) * 16

        block = ctx.enter_context(nc.Block())

        def steps(eng, one, between=()):
            def at(i, c):
                pairs = [Pair(i, c - k) for k in range(STAGES)]
                one([q if q.exists() else None for q in pairs])
            fill = STAGES + 1 + (PAIRS - STAGES - 1) % TURNS
            for t in range(fill):
                at(t // 2, t % 2)
                if t < len(between):
                    between[t]()
            with eng.Fori(fill // 2, (PAIRS - TURNS) // 2 + 1, TURNS // 2) as i:
                for c in range(TURNS):
                    at(i, c)
            for t in range(PAIRS, PAIRS + STAGES - 1):
                at(t // 2, t % 2)

        def no_setup():
            pass

        DVE_ADJ, DVE_MASK, DVE_MASK_BF, DVE_WH, DVE_DEG, DVE_LAST = 4, 5, 6, 7, 8, 9
        DOTS_HEADS, DOTS_ALL = 2 * C * H, 2 * C * H + 2 * K2
        ACT_WH, ACT_WO, ACT_LAST = 1, 3, 5
        POOL_WO = 2

        @block.sync
        def _(sp):
            for c in range(C):
                sp.dma_start(wh[:, c, :, :], w_heads[:, c * P:(c + 1) * P, :].rearrange("h f o -> f h o")).then_inc(heads_in, 16)
            sp.dma_start(ah_bc[:, :, :], a_heads.partition_broadcast(P)).then_inc(heads_in, 16)

            def load_later_weights():
                sp.dma_start(wo[:, :, :], w_out.rearrange("(k f) o -> f k o", f=P)).then_inc(out_in, 16)
                sp.dma_start(ao_bc[:, :, :], a_out.rearrange("(j o) -> j o", j=2).partition_broadcast(P)).then_inc(out_in, 16)
                sp.dma_start(l1w_sb[:, :, :], l1w.rearrange("(k o) d -> o k d", o=P)).then_inc(last_in, 16)
                sp.dma_start(w1_sb[:, :, :], w1.rearrange("(k f) o -> f k o", f=P)).then_inc(ffn_in, 16)
                sp.dma_start(w2_sb[:, :, :], w2.rearrange("(k f) o -> f k o", f=P)).then_inc(ffn_in, 16)

            def pair_of(ap, q):
                return ap[bass.ds(q.i * 4 + q.c * 2, 2), :, :].rearrange("b n f -> n b f")

            def load_x(p):
                wait(sp, "h_ready", p, lag=2)
                sp.dma_start(xa[p.e][:, :, :], pair_of(x, p)).then_inc(x_in[p.e], 16)

            def load_residual(p):
                wait(sp, "x_plus_beta", p, lag=2)
                sp.dma_start(xr[p.e][:, :, :], pair_of(x, p)).then_inc(r_in[p.e], 16)

            def store(p):
                wait(sp, "result_ready", p)
                sp.dma_start(pair_of(out, p), res[p.e][:, :, :]).then_inc(stored[p.e], 16)

            def one(pairs):
                if p := pairs[0]:
                    load_x(p)
                if p := pairs[2]:
                    load_residual(p)
                if p := pairs[5]:
                    store(p)
            steps(sp, one, [load_later_weights])
            for e in range(2):
                sp.wait_ge(stored[e], PAIRS // 2 * 16)

        @block.gpsimd
        def _(pool):
            pool.dma_start(adj_i[:, :], adj).then_inc(adj_in, 16)
            pool.dma_start(b1_col[:, :], b1.rearrange("(k d) -> d k", d=P), allow_slow_non_contiguous=True).then_inc(consts_in, 16)
            pool.dma_start(b2_col[:, :], b2.rearrange("(k d) -> d k", d=P), allow_slow_non_contiguous=True).then_inc(consts_in, 16)
            for dst, src in ((gamma_bc, gamma), (beta_bc, beta), (l1b_bc, l1b)):
                pool.dma_start(dst[:, :], src.partition_broadcast(P)).then_inc(consts_in, 16)
            pool.memset(ident[:, :], 0.0).then_inc(memset_done, 1)
            pool.memset(rowsel[:, :, :], 0.0).then_inc(memset_done, 1)
            pool.memset(minus_half[:, :], -0.5).then_inc(memset_done, 1)
            pool.memset(eps[:, :], EPS).then_inc(memset_done, 1)
            pool.wait_ge(memset_done, 1)
            pool.affine_select(out=ident[:, :], in_=ident[:, :], compare_op=ALU.not_equal, fill=1.0,
                               base=0, pattern=[[-1, P]], channel_multiplier=1).then_inc(ident_ready, 1)
            pool.wait_ge(ident_ready, 1)
            pool.tensor_copy(ident_bf[:, :], ident[:, :]).then_inc(ident_ready, 1)

            def row_selectors():
                pool.wait_ge(memset_done, 2)
                for n, g in enumerate(G3):
                    if n:
                        pool.wait_ge(rowsel_ready, n)
                    pool.affine_select(out=rowsel[:, :, :], in_=rowsel[:, :, :], compare_op=ALU.not_equal, fill=1.0,
                                       base=-g, pattern=[[-1, 4 * H], [0, P]], channel_multiplier=1).then_inc(rowsel_ready, 1)

            pool.wait_ge(memset_done, 4)

            def rstd(name, p, mv, ve, rs):
                wait(pool, name + "_moments", p)
                pool.tensor_tensor(ve[p.e][:, :], mv[p.e][:, :, 1], eps[:, :], ALU.add).then_inc(S[name + "_variance"], 1)
                wait(pool, name + "_variance", p)
                pool.tensor_tensor(rs[p.e][:, :], ve[p.e][:, :], minus_half[:, :], ALU.pow).then_inc(S[name + "_rstd"], 1)

            def h2_low(p, u):
                wait(pool, "heads_hi", p, u + 1)
                pool.tensor_tensor(h2_lo[:, u, :, :].rearrange("p c n -> p (c n)"), h2v[u % 2][:, :],
                                   h2_hi[:, u, :, :].rearrange("p c n -> p (c n)").bitcast(F32), ALU.subtract).then_inc(S["heads_lo"], 1)

            def soft_mask(p, b):
                if p.is_first() and b == 0:
                    pool.wait_ge(dve_setup, DVE_MASK)
                wait(pool, "scores_leaky", p, b + 1)
                pool.tensor_tensor(zt[:, b, :, :], zt[:, b, :, :], mask[:, :].unsqueeze(1).broadcast_to([P, H, P]), ALU.add)\
                    .then_inc(S["scores_masked"], 1)

            def scale2(p):
                if p.is_first():
                    pool.wait_ge(consts_in, 80)
                wait(pool, "normal2_ready", p)
                pool.tensor_tensor(lt[p.e][:, :, :], lt[p.e][:, :, :],
                                  gamma_bc[:, :].unsqueeze(1).broadcast_to([P, 2, F]), ALU.mult).then_inc(S["normal2_scaled"], 1)

            def soft(p, b):
                wait(pool, "sums_inverted", p, b + 1)
                if b == 0:
                    wait(pool, "probs_transposed", p, lag=1)
                pool.tensor_tensor(zn[:, b, :, :], zp[:, b, :, :],
                                   zr[p.e][:, b, :].unsqueeze(2).broadcast_to([P, H, P]), ALU.mult).then_inc(S["probs_ready"], 1)

            def add_beta(p):
                if p.is_first():
                    pool.wait_ge(consts_in, 80)
                pool.wait_ge(r_in[p.e], half(p))
                wait(pool, "x2_ready", p, lag=1)
                pool.tensor_tensor(xb[p.e][:, :, :], xr[p.e][:, :, :],
                                   beta_bc[:, :].unsqueeze(1).broadcast_to([P, 2, F]), ALU.add).then_inc(S["x_plus_beta"], 1)

            def add_bias(p):
                if p.is_first():
                    pool.wait_ge(dve_setup, DVE_DEG)
                wait(pool, "x2_ready", p)
                wait(pool, "result_ready", p, lag=1)
                pool.tensor_tensor(x2d[p.e][:, :, :], x2[p.e][:, :, :],
                                   deg_bias[:, :].unsqueeze(1).broadcast_to([P, 2, F]), ALU.add).then_inc(S["x2_plus_bias"], 1)

            def rstd1(p):
                rstd("x", p, a_mv, a_ve, a_rs)

            def rstd2(p):
                rstd("ffn", p, b_mv, b_ve, b_rs)

            def rstd3(p):
                rstd("x2", p, c_mv, c_ve, c_rs)

            def h_low(p):
                wait(pool, "h_hi", p)
                pool.tensor_tensor(h_lo[p.e][:, :, :], h[p.e][:, :, :], h_hi[p.e][:, :, :].bitcast(F32),
                                   ALU.subtract).then_inc(S["h_lo"], 1)

            def h3_low(p):
                wait(pool, "h3_hi", p)
                pool.tensor_tensor(h3_lo[:, :, :], h3[p.e][:, :, :], h3_hi[:, :, :].bitcast(F32),
                                   ALU.subtract).then_inc(S["h3_lo"], 1)

            def one(pairs):
                if p := pairs[2]:
                    soft(p, 0)
                if p := pairs[3]:
                    h2_low(p, 1)
                    h2_low(p, 2)
                    h2_low(p, 3)
                if p := pairs[2]:
                    soft(p, 1)
                if p := pairs[4]:
                    rstd2(p)
                    scale2(p)
                if p := pairs[0]:
                    rstd1(p)
                if p := pairs[4]:
                    rstd3(p)
                if p := pairs[3]:
                    add_beta(p)
                if p := pairs[1]:
                    h_low(p)
                if p := pairs[4]:
                    h3_low(p)
                    add_bias(p)
                if p := pairs[1]:
                    soft_mask(p, 0)
                if p := pairs[2]:
                    h2_low(p, 0)
                if p := pairs[1]:
                    soft_mask(p, 1)
            def low_w_out():
                pool.wait_ge(act_setup, ACT_WO)
                pool.tensor_tensor(wo_lo[:, :, 0:F], wo[:, :, :], wo_hi[:, :, 0:F].bitcast(F32), ALU.subtract).then_inc(pool_setup, 1)
                pool.tensor_tensor(wo_lo[:, :, F:WO], wo_a[:, :, :], wo_hi[:, :, F:WO].bitcast(F32), ALU.subtract)\
                    .then_inc(pool_setup, 1)

            steps(pool, one, [row_selectors, low_w_out])

        @block.vector
        def _(dve):
            own, chain = sem("dve_chain"), [0]

            def after(ins):
                chain[0] += 1
                ins.then_inc(own, 1)
                dve.wait_ge(own, chain[0])

            dots = [0]

            def dot(a, b, total):
                if dots[0] >= 4:
                    dve.wait_ge(dotted, dots[0] - 3)
                slot = res[dots[0] // 2 % 2][:, dots[0] % 2, :]
                dots[0] += 1
                dve.scalar_tensor_tensor(slot, a, 1.0, b, ALU.mult, ALU.mult, accum_out=total).then_inc(dotted, 1)

            dve.memset(f_rep[0][:, :], 0.0).then_inc(dve_setup, 1)
            dve.memset(f2_rep[0][:, :], 0.0).then_inc(dve_setup, 1)
            dve.memset(f2_rep[1][:, :], 0.0).then_inc(dve_setup, 1)
            dve.wait_ge(adj_in, 16)
            dve.tensor_copy(adj_f[:, :], adj_i[:, :]).then_inc(dve_setup, 1)
            dve.wait_ge(dve_setup, DVE_ADJ)
            dve.tensor_scalar(mask[:, :], adj_f[:, :], 0.0, NEG, ALU.is_le, ALU.mult).then_inc(dve_setup, 1)
            dve.tensor_scalar(mask_bf[:, :, :], adj_f[:, :].unsqueeze(1).broadcast_to([P, 2, P]), 0.0, NEG,
                              ALU.is_le, ALU.mult).then_inc(dve_setup, 1)

            def heads_weights():
                dve.wait_ge(heads_in, 48)
                for c in range(C):
                    for hd in range(H):
                        for j in range(2):
                            dot(wh[:, c, hd, :], ah_bc[:, hd, j * F:(j + 1) * F], wa[:, c, j, hd:hd + 1])
                dve.wait_ge(out_in, 32)
                for k in range(K2):
                    for j in range(2):
                        dot(wo[:, k, :], ao_bc[:, j, :], wo_a[:, k, j:j + 1])

            def middle_weights():
                dve.wait_ge(act_setup, ACT_WH)
                dve.tensor_tensor(wh_lo[:, :, :, :], wh[:, :, :, :], wh_hi[:, :, :, :].bitcast(F32), ALU.subtract)\
                   .then_inc(dve_setup, 1)
                after(dve.reduce_sum(deg[:, :], adj_f[:, :], axis=X))
                dve.wait_ge(consts_in, 80)
                dve.wait_ge(ident_ready, 2)
                dve.tensor_scalar(adj_deg[:, 1, :], ident[:, :], deg[:, 0:1], None, ALU.mult)
                dve.tensor_scalar(deg_bias[:, :], l1b_bc[:, :], deg[:, 0:1], None, ALU.mult).then_inc(dve_setup, 1)

            def later_weights():
                dve.wait_ge(pe_setup, 1)
                dve.tensor_copy(adj_deg[:, 0, :], ps_z[:, 0, 0:P])
                dve.wait_ge(act_setup, ACT_LAST)
                for s in range(2):
                    last = dve.tensor_tensor(l1w_lo[:, s, :, :].rearrange("p c o -> p (c o)"), ps_g[:, 2 + s, :],
                                             l1w_hi[:, s, :, :].rearrange("p c o -> p (c o)").bitcast(F32), ALU.subtract)
                last.then_inc(dve_setup, 1)

            def stats(name, p, src, st):
                for b in range(2):
                    dve.bn_stats(st[p.e][:, b, :], src(b)).then_inc(S[name + "_stats"], 1)

            def mean_var(name, p, st, mv):
                for b in range(2):
                    wait(dve, name + "_stats", p, b + 1)
                    dve.nop(nofuse=True)
                    dve.bn_aggr(mv[p.e][:, b, :], st[p.e][:, b, :]).then_inc(S[name + "_moments"], 1)

            def shift(name, p, mv, rs, nm):
                wait(dve, name + "_rstd", p)
                dve.scalar_tensor_tensor(nm[p.e][:, :], mv[p.e][:, :, 0], -1.0, rs[p.e][:, :], ALU.mult, ALU.mult)\
                   .then_inc(S[name + "_shift"], 1)

            def gh_low(p, u):
                b, c = u // 2, u % 2
                wait(dve, "gh_hi", p, u + 1)
                dve.tensor_tensor(gh_lo[:, c, :, b, :], ps_g[:, u % 2, :].rearrange("p (h n) -> p h n", h=H),
                                  gh_hi[:, c, :, b, :].bitcast(F32), ALU.subtract).then_inc(S["gh_lo"], 1)

            def less_first(name, p, psum, parts, rest):
                wait(dve, name + "_first", p)
                dve.tensor_tensor(rest[p.e][64:P, :], psum[64:P, :], parts[p.e][64:P, :], ALU.subtract)\
                   .then_inc(S[name + "_rest"], 1)

            def second(name, p, parts, rest):
                wait(dve, name + "_rest", p)
                dve.tensor_copy(parts[p.e][64:P, :], rest[p.e][64:P, :]).then_inc(S[name + "_second"], 1)

            def third(name, p, parts, rest):
                wait(dve, name + "_second", p)
                dve.tensor_tensor(parts[p.e][96:P, :], rest[p.e][96:P, :], parts[p.e][96:P, :], ALU.subtract)\
                   .then_inc(S[name + "_third"], 1)

            def f_cols(p):
                wait(dve, "cols_done", p)
                wait(dve, "rows_done", p, lag=1)
                dve.tensor_copy(f_rep[p.e][:, 32:P].rearrange("p (g r) -> p g r", r=32)[:, :, 0:4 * H],
                                ps_x[:, 0, 0:4 * H].unsqueeze(1).broadcast_to([P, 3, 4 * H])).then_inc(S["cols_copied"], 1)

            def f_less_first(p):
                less_first("rows", p, ps_x[:, 0, 0:P], f_parts, f_rest)

            def f_second(p):
                second("rows", p, f_parts, f_rest)

            def f_third(p):
                third("rows", p, f_parts, f_rest)

            def g_first(p):
                wait(dve, "rows2_done", p)
                wait(dve, "scores2_done", p, lag=2)
                dve.tensor_copy(g_parts[p.e][:, :], ps_z[:, 0, 0:P]).then_inc(S["rows2_first"], 1)

            def g_less_first(p):
                less_first("rows2", p, ps_z[:, 0, 0:P], g_parts, g_rest)

            def g_second(p):
                second("rows2", p, g_parts, g_rest)

            def g_third(p):
                third("rows2", p, g_parts, g_rest)

            def elu_min(p, u):
                i = u % 2
                wait(dve, "heads_exp", p, u + 1)
                dve.tensor_scalar(h2e[i][:, :], h2e[i][:, :], 1.0, 0.0, ALU.subtract, ALU.min).then_inc(S["heads_min"], 1)

            def elu(p, u):
                i = u % 2
                wait(dve, "heads_min", p, u + 1)
                if u >= 2:
                    wait(dve, "heads_lo", p, u - 1)
                else:
                    wait(dve, "heads_lo", p, u + 3, lag=1)
                dve.tensor_tensor(h2v[i][:, :], h2e[i][:, :], ps_g[:, u % 2, :], ALU.max).then_inc(S["heads_elu"], 1)

            def soft_leaky(p, b):
                wait(dve, "scores_copied", p, b + 1)
                dve.scalar_tensor_tensor(zt[:, b, :, :], zt[:, b, :, :], 0.01, zt[:, b, :, :],
                                         ALU.mult, ALU.max).then_inc(S["scores_leaky"], 1)

            def soft_max(p, b):
                wait(dve, "scores_masked", p, b + 1)
                dve.tensor_reduce(zm[p.e][:, b, :], zt[:, b, :, :], X, ALU.max, negate=True).then_inc(S["scores_max"], 1)

            def soft_sum(p, b):
                wait(dve, "exps_done", p, H * (b + 1))
                dve.reciprocal(zr[p.e][:, b, :], zs[p.e][:, b, :]).then_inc(S["sums_inverted"], 1)

            def wh2_scores(p, b):
                wait(dve, "wh2_copied", p, b + 1)
                wait(dve, "rows2_done", p, lag=2)
                dve.tensor_copy(f2_rep[p.e][:, 32:P].rearrange("p (g r) -> p g r", r=32)[:, :, b:b + 3:2],
                                ps_g[:, 2 + b, F:WO].unsqueeze(1).broadcast_to([P, 3, 2])).then_inc(S["wh2_scores_copied"], 1)

            def soft_leaky2(p):
                wait(dve, "scores2_copied", p)
                dve.scalar_tensor_tensor(yt[p.e][:, :, :], yt[p.e][:, :, :], 0.01, yt[p.e][:, :, :],
                                         ALU.mult, ALU.max).then_inc(S["scores2_leaky"], 1)

            def soft_max2(p):
                wait(dve, "scores2_leaky", p)
                dve.tensor_reduce(ym[p.e][:, :], yt[p.e][:, :, :], X, ALU.max, negate=True).then_inc(S["scores2_max"], 1)

            def soft_sum2(p):
                wait(dve, "exps2_done", p)
                dve.reciprocal(yr[p.e][:, :], ys[p.e][:, :]).then_inc(S["sums2_inverted"], 1)

            def soft2(p):
                wait(dve, "sums2_inverted", p)
                wait(dve, "probs2_transposed", p, lag=1)
                dve.tensor_tensor(yn[p.e][:, :, :], yp[p.e][:, :, :],
                                  yr[p.e][:, :].unsqueeze(2).broadcast_to([P, 2, P]), ALU.mult).then_inc(S["probs2_ready"], 1)

            def out_min(p):
                wait(dve, "out_exp", p)
                dve.tensor_scalar(oe[p.e][:, :, :], oe[p.e][:, :, :], 1.0, 0.0, ALU.subtract, ALU.min).then_inc(S["out_min"], 1)

            def out_elu(p):
                wait(dve, "out_min", p)
                wait(dve, "ffn_transposed", p, lag=1)
                dve.tensor_tensor(ov[p.e][:, :, :], oe[p.e][:, :, :],
                                  ps_z[:, 1, :].rearrange("p (c n) -> p c n", c=C), ALU.max).then_inc(S["out_elu"], 1)

            def add_out(p, oc):
                if p.is_first() and oc == 0:
                    dve.wait_ge(consts_in, 80)
                wait(dve, "ffn_done", p)
                dve.scalar_tensor_tensor(ov[p.e][:, oc, :], ps_z[:, 1, oc * 2 * P:(oc + 1) * 2 * P], b2_col[:, oc:oc + 1],
                                         ov[p.e][:, oc, :], ALU.add, ALU.add).then_inc(S["ffn_plus_out"], 1)

            def norm2_stats(p):
                wait(dve, "ffn_transposed", p)
                stats("ffn", p, lambda b: ps_z[:, 0, b * F:(b + 1) * F], b_st)

            def norm2_var(p):
                mean_var("ffn", p, b_st, b_mv)

            def norm2_shift(p):
                shift("ffn", p, b_mv, b_rs, b_nm)

            def residual2(p):
                wait(dve, "normal2_scaled", p)
                wait(dve, "x_plus_beta", p)
                wait(dve, "h3_ready", p, lag=1)
                wait(dve, "x2_plus_bias", p, lag=1)
                dve.tensor_tensor(x2[p.e][:, :, :], lt[p.e][:, :, :], xb[p.e][:, :, :], ALU.add).then_inc(S["x2_ready"], 1)

            def norm3_stats(p):
                wait(dve, "x2_ready", p)
                stats("x2", p, lambda b: x2[p.e][:, b, :], c_st)

            def norm3_var(p):
                mean_var("x2", p, c_st, c_mv)

            def norm3_shift(p):
                shift("x2", p, c_mv, c_rs, c_nm)

            def at_low(p, b):
                wait(dve, "at_hi", p, b + 1)
                dve.tensor_tensor(at_lo[p.e][:, b, :], ps_x[:, b, :], at_hi[p.e][:, b, :].bitcast(F32),
                                  ALU.subtract).then_inc(S["at_lo"], 1)

            def norm1_stats(p):
                dve.wait_ge(x_in[p.e], half(p))
                stats("x", p, lambda b: xa[p.e][:, b, :], a_st)

            def norm1_var(p):
                mean_var("x", p, a_st, a_mv)

            def norm1_shift(p):
                shift("x", p, a_mv, a_rs, a_nm)

            def gd_low(p, b):
                wait(dve, "gd_hi", p, b + 1)
                dve.tensor_tensor(gd_lo[:, b, :, :, :], ps_x[:, b, :].rearrange("p (c s n) -> p c s n", c=C, s=2),
                                  gd_hi[:, b, :, :, :].bitcast(F32), ALU.subtract).then_inc(S["gd_lo"], 1)

            def result(p):
                wait(dve, "last_done", p)
                wait(dve, "x2_plus_bias", p)
                if p.lagged(2).exists():
                    dve.wait_ge(stored[p.e], half(p, 2))
                dve.tensor_tensor(res[p.e][:, :, :], x2d[p.e][:, :, :],
                                  ps_x[:, 0, :].rearrange("p (b o) -> p b o", b=2), ALU.add).then_inc(S["result_ready"], 1)

            def one(pairs):
                if p := pairs[2]:
                    soft_sum(p, 0)
                if p := pairs[3]:
                    elu(p, 2)
                if p := pairs[2]:
                    soft_max(p, 1)
                if p := pairs[3]:
                    elu_min(p, 3)
                    elu(p, 3)
                if p := pairs[4]:
                    add_out(p, 0)
                    add_out(p, 1)
                if p := pairs[2]:
                    soft_sum(p, 1)
                    at_low(p, 0)
                if p := pairs[0]:
                    norm1_stats(p)
                if p := pairs[4]:
                    norm2_stats(p)
                    norm2_var(p)
                if p := pairs[5]:
                    gd_low(p, 1)
                if p := pairs[4]:
                    norm2_shift(p)
                if p := pairs[2]:
                    gh_low(p, 0)
                    gh_low(p, 1)
                    at_low(p, 1)
                if p := pairs[0]:
                    norm1_var(p)
                if p := pairs[3]:
                    wh2_scores(p, 0)
                if p := pairs[4]:
                    residual2(p)
                if p := pairs[3]:
                    wh2_scores(p, 1)
                if p := pairs[4]:
                    norm3_stats(p)
                if p := pairs[3]:
                    g_first(p)
                if p := pairs[1]:
                    f_cols(p)
                if p := pairs[3]:
                    g_less_first(p)
                if p := pairs[4]:
                    norm3_var(p)
                if p := pairs[3]:
                    g_second(p)
                    g_third(p)
                if p := pairs[2]:
                    gh_low(p, 2)
                if p := pairs[4]:
                    norm3_shift(p)
                if p := pairs[2]:
                    gh_low(p, 3)
                if p := pairs[3]:
                    soft_leaky2(p)
                    soft_max2(p)
                if p := pairs[5]:
                    result(p)
                if p := pairs[3]:
                    soft_sum2(p)
                    soft2(p)
                if p := pairs[1]:
                    f_less_first(p)
                    f_second(p)
                    f_third(p)
                if p := pairs[2]:
                    elu_min(p, 0)
                    elu(p, 0)
                    elu_min(p, 1)
                if p := pairs[1]:
                    soft_leaky(p, 0)
                if p := pairs[2]:
                    elu(p, 1)
                if p := pairs[3]:
                    out_min(p)
                if p := pairs[0]:
                    norm1_shift(p)
                if p := pairs[3]:
                    out_elu(p)
                if p := pairs[1]:
                    soft_max(p, 0)
                    soft_leaky(p, 1)
                if p := pairs[4]:
                    gd_low(p, 0)
                if p := pairs[2]:
                    elu_min(p, 2)
            steps(dve, one, [heads_weights, middle_weights, later_weights])

        @block.scalar
        def _(act):
            def heads_weights():
                act.wait_ge(heads_in, 48)
                act.activation(wh_hi[:, :, :, :], wh[:, :, :, :], ACT.Copy).then_inc(act_setup, 1)

            def middle_weights():
                act.wait_ge(dotted, DOTS_ALL)
                act.activation(wo_hi[:, :, 0:F], wo[:, :, :], ACT.Copy).then_inc(act_setup, 1)
                act.activation(wo_hi[:, :, F:WO], wo_a[:, :, :], ACT.Copy).then_inc(act_setup, 1)

            def later_weights():
                act.wait_ge(pe_setup, 1)
                for s in range(2):
                    act.activation(l1w_hi[:, s, :, :].rearrange("p c o -> p (c o)"), ps_g[:, 2 + s, :], ACT.Copy)\
                       .then_inc(act_setup, 1)

            def gh_high(p, u):
                b, c = u // 2, u % 2
                wait(act, "gh_done", p, u + 1)
                if u == 0:
                    wait(act, "heads_done", p, lag=1)
                act.activation(gh_hi[:, c, :, b, :], ps_g[:, u % 2, :].rearrange("p (h n) -> p h n", h=H),
                               ACT.Copy).then_inc(S["gh_hi"], 1)

            def elu_exp(p, u):
                if u >= 2:
                    wait(act, "heads_elu", p, u - 1)
                else:
                    wait(act, "heads_elu", p, u + 3, lag=1)
                wait(act, "heads_done", p, u + 1)
                act.activation(h2e[u % 2][:, :], ps_g[:, u % 2, :], ACT.Exp).then_inc(S["heads_exp"], 1)

            def score_copy(p, b):
                wait(act, "scores_done", p, b + 1)
                act.activation(zt[:, b, :, :], ps_x[:, b, :].rearrange("p (h m) -> p h m", h=H), ACT.Copy)\
                   .then_inc(S["scores_copied"], 1)

            def soft_exp(p, b):
                wait(act, "scores_masked", p, b + 1)
                wait(act, "scores_max", p, b + 1)
                if b == 0:
                    wait(act, "probs_ready", p, lag=1)
                for hd in range(H):
                    act.activation(zp[:, b, hd, :], zt[:, b, hd, :], ACT.Exp, bias=zm[p.e][:, b, hd:hd + 1],
                                   accum_out=zs[p.e][:, b, hd:hd + 1]).then_inc(S["exps_done"], 1)

            def wh2_copy(p, b):
                wait(act, "wh2_done", p, b + 1)
                wait(act, "out_done", p, lag=1)
                act.activation(wh2[p.e][:, b, :], ps_g[:, 2 + b, 0:F], ACT.Copy).then_inc(S["wh2_copied"], 1)

            def normal(name, p, dst, src, rs, nm, func, done):
                wait(act, name + "_shift", p)
                for b in range(2):
                    act.activation(dst[p.e][:, b, :], src(b), func, bias=nm[p.e][:, b:b + 1],
                                   scale=rs[p.e][:, b:b + 1]).then_inc(S[done], 1)

            def ht_copy(p):
                wait(act, "ht_done", p)
                wait(act, "cols_done", p, lag=1)
                act.activation(ht[p.e][:, :, :], ps_x[:, 1, :].rearrange("p (c n) -> p c n", c=C), ACT.Copy)\
                   .then_inc(S["ht_copied"], 1)

            def f_first(p):
                wait(act, "rows_done", p)
                wait(act, "scores_done", p, lag=1)
                act.activation(f_parts[p.e][:, :], ps_x[:, 0, 0:P], ACT.Copy).then_inc(S["rows_first"], 1)

            def score_copy2(p):
                wait(act, "scores2_done", p)
                act.activation(yt[p.e][:, :, :], ps_z[:, 1, 0:2 * P].rearrange("p (b m) -> p b m", b=2), ACT.Copy)\
                   .then_inc(S["scores2_copied"], 1)

            def h2_high(p, u):
                wait(act, "heads_elu", p, u + 1)
                if u == 0:
                    wait(act, "wh2_done", p, lag=1)
                act.activation(h2_hi[:, u, :, :].rearrange("p c n -> p (c n)"), h2v[u % 2][:, :], ACT.Copy).then_inc(S["heads_hi"], 1)

            def h_high(p):
                wait(act, "h_ready", p)
                wait(act, "gh_done", p, lag=2)
                act.activation(h_hi[p.e][:, :, :], h[p.e][:, :, :], ACT.Copy).then_inc(S["h_hi"], 1)

            def h3_high(p):
                wait(act, "h3_ready", p)
                wait(act, "gather_done", p, lag=1)
                act.activation(h3_hi[:, :, :], h3[p.e][:, :, :], ACT.Copy).then_inc(S["h3_hi"], 1)

            def soft_exp2(p):
                wait(act, "scores2_max", p)
                wait(act, "probs2_ready", p, lag=1)
                for b in range(2):
                    act.activation(yp[p.e][:, b, :], yt[p.e][:, b, :], ACT.Exp, bias=ym[p.e][:, b:b + 1],
                                   accum_out=ys[p.e][:, b:b + 1]).then_inc(S["exps2_done"], 1)

            def a2_copy(p):
                wait(act, "probs2_transposed", p)
                wait(act, "out_done", p, lag=1)
                act.activation(a2t[p.e][:, :, :], ps_z[:, 0, 0:2 * P].rearrange("p (b m) -> p b m", b=2), ACT.Copy)\
                   .then_inc(S["probs2_copied"], 1)

            def out_exp(p):
                wait(act, "out_done", p)
                wait(act, "out_elu", p, lag=1)
                act.activation(oe[p.e][:, :, :], ps_z[:, 1, :].rearrange("p (c n) -> p c n", c=C), ACT.Exp)\
                   .then_inc(S["out_exp"], 1)

            def hidden_relu(p):
                if p.is_first():
                    act.wait_ge(consts_in, 80)
                wait(act, "hidden_done", p)
                wait(act, "ffn_done", p, lag=1)
                for c in range(C):
                    act.activation(hid[p.e][:, c, :], ps_z[:, 0, c * 2 * P:(c + 1) * 2 * P], ACT.Relu,
                                   bias=b1_col[:, c:c + 1]).then_inc(S["hidden_ready"], 1)

            def norm2(p):
                wait(act, "x2_ready", p, lag=1)
                normal("ffn", p, lt, lambda b: ps_z[:, 0, b * F:(b + 1) * F], b_rs, b_nm, ACT.Identity, "normal2_ready")

            def norm3(p):
                wait(act, "h3_lo", p, lag=1)
                normal("x2", p, h3, lambda b: x2[p.e][:, b, :], c_rs, c_nm, ACT.Relu, "h3_ready")

            def norm1(p):
                wait(act, "h_lo", p, lag=2)
                wait(act, "ht_done", p, lag=2)
                normal("x", p, h, lambda b: xa[p.e][:, b, :], a_rs, a_nm, ACT.Relu, "h_ready")

            def at_high(p, b):
                wait(act, "probs_transposed", p, b + 1)
                wait(act, "gh_done", p, lag=2)
                act.activation(at_hi[p.e][:, b, :], ps_x[:, b, :], ACT.Copy).then_inc(S["at_hi"], 1)

            def gd_high(p, b):
                wait(act, "gather_done", p, b + 1)
                wait(act, "last_done", p, lag=1)
                act.activation(gd_hi[:, b, :, :, :], ps_x[:, b, :].rearrange("p (c s n) -> p c s n", c=C, s=2),
                               ACT.Copy).then_inc(S["gd_hi"], 1)

            def one(pairs):
                if p := pairs[2]:
                    soft_exp(p, 0)
                if p := pairs[4]:
                    hidden_relu(p)
                if p := pairs[3]:
                    elu_exp(p, 3)
                    h2_high(p, 2)
                if p := pairs[2]:
                    soft_exp(p, 1)
                    at_high(p, 0)
                if p := pairs[3]:
                    h2_high(p, 3)
                if p := pairs[5]:
                    gd_high(p, 1)
                if p := pairs[1]:
                    norm1(p)
                    h_high(p)
                if p := pairs[2]:
                    gh_high(p, 0)
                    gh_high(p, 1)
                if p := pairs[4]:
                    norm2(p)
                if p := pairs[2]:
                    at_high(p, 1)
                if p := pairs[3]:
                    wh2_copy(p, 0)
                    wh2_copy(p, 1)
                if p := pairs[1]:
                    ht_copy(p)
                if p := pairs[2]:
                    gh_high(p, 2)
                    gh_high(p, 3)
                if p := pairs[3]:
                    score_copy2(p)
                if p := pairs[4]:
                    norm3(p)
                if p := pairs[3]:
                    soft_exp2(p)
                if p := pairs[1]:
                    f_first(p)
                if p := pairs[4]:
                    h3_high(p)
                if p := pairs[2]:
                    elu_exp(p, 0)
                if p := pairs[3]:
                    a2_copy(p)
                if p := pairs[2]:
                    elu_exp(p, 1)
                if p := pairs[1]:
                    score_copy(p, 0)
                if p := pairs[2]:
                    h2_high(p, 0)
                if p := pairs[3]:
                    out_exp(p)
                if p := pairs[4]:
                    gd_high(p, 0)
                if p := pairs[2]:
                    h2_high(p, 1)
                if p := pairs[1]:
                    score_copy(p, 1)
                if p := pairs[2]:
                    elu_exp(p, 2)
            steps(act, one, [heads_weights, middle_weights, later_weights])

        @block.tensor
        def _(pe):
            pe.wait_ge(ident_ready, 2)

            def later_weights():
                pe.wait_ge(last_in, 16)
                pe.wait_ge(dve_setup, DVE_ADJ)
                pe.transpose(ps_z[:, 0, 0:P], adj_f[:, :], ident[:, :])
                for s in range(2):
                    for c in range(C):
                        for k in range(C):
                            last = pe.transpose(ps_g[:, 2 + s, c * F + k * P:c * F + (k + 1) * P],
                                                l1w_sb[:, k, s * F + c * P:s * F + (c + 1) * P], ident[:, :])
                last.then_inc(pe_setup, 1)

            def wait_bank(p, *before):
                for name, k, lag in before:
                    if p.lagged(lag).exists():
                        wait(pe, name, p, k, lag=lag)
                        return

            def mm(out_, lhs, rhs, start, stop):
                return pe.matmul(out_, lhs, rhs, start=start, stop=stop)

            def three(out_, lhs, rhs, first, last):
                mm(out_, lhs[0], rhs[0], first, False)
                mm(out_, lhs[0], rhs[1], False, False)
                return mm(out_, lhs[1], rhs[0], False, last)

            def gh_unit(p, u):
                b, c = u // 2, u % 2
                if u == 0:
                    wait(pe, "h_lo", p)
                wait(pe, "at_lo", p, b + 1)
                if u == 0:
                    wait_bank(p, ("heads_elu", 3, 1))
                if u == 1:
                    wait_bank(p, ("heads_elu", 4, 1))
                if u == 2:
                    wait_bank(p, ("gh_lo", 1, 0))
                if u == 3:
                    wait_bank(p, ("gh_lo", 2, 0))
                cols = slice(c * P, (c + 1) * P)
                three(ps_g[:, u % 2, :], (h_hi[p.e][:, b, cols], h_lo[p.e][:, b, cols]),
                      (at_hi[p.e][:, b, :], at_lo[p.e][:, b, :]), True, True).then_inc(S["gh_done"], 1)

            def h2_unit(p, u, oc):
                if p.is_first() and u == oc == 0:
                    pe.wait_ge(dve_setup, DVE_WH)
                if u == oc == 0:
                    wait(pe, "gh_lo", p)
                if u == 2 and oc == 0:
                    wait_bank(p, ("heads_elu", 1, 0))
                if u == 3 and oc == 0:
                    wait_bank(p, ("heads_elu", 2, 0))
                cols = slice(oc * P, (oc + 1) * P)
                for c in range(C):
                    last = three(ps_g[:, u % 2, oc * 2 * P:(oc + 1) * 2 * P],
                                 (wh_hi[:, c, u, cols], wh_lo[:, c, u, cols]),
                                 (gh_hi[:, c, u, :, :].rearrange("p b n -> p (b n)"),
                                  gh_lo[:, c, u, :, :].rearrange("p b n -> p (b n)")), c == 0, c == C - 1)
                if oc == C - 1:
                    last.then_inc(S["heads_done"], 1)

            def wh2_part(p, b, hd):
                if p.is_first() and b == hd == 0:
                    pe.wait_ge(pool_setup, POOL_WO)
                    pe.wait_ge(dve_setup, DVE_LAST)
                if hd == 0:
                    wait(pe, "wh2_scores_copied", p, b + 1, lag=1)
                rows = slice(b * P, (b + 1) * P)
                if b == 0:
                    wait(pe, "heads_lo", p, hd + 1)
                for c in range(C):
                    k = hd * C + c
                    last = three(ps_g[:, 2 + b, 0:WO], (h2_hi[:, hd, c, rows], h2_lo[:, hd, c, rows]),
                                 (wo_hi[:, k, :], wo_lo[:, k, :]), k == 0, k == K2 - 1)
                if hd == H - 1:
                    last.then_inc(S["wh2_done"], 1)

            def h_transposes(p):
                wait(pe, "h_ready", p)
                wait_bank(p, ("at_lo", 2, 1))
                for c in range(C):
                    for b in range(2):
                        last = pe.transpose(ps_x[:, 1, (c * 2 + b) * P:(c * 2 + b + 1) * P],
                                            h[p.e][:, b, c * P:(c + 1) * P], ident[:, :])
                last.then_inc(S["ht_done"], 1)

            def score_cols(p):
                if p.is_first():
                    pe.wait_ge(dotted, DOTS_HEADS)
                wait(pe, "ht_copied", p)
                wait_bank(p, ("at_lo", 1, 1))
                for b in range(2):
                    for c in range(C):
                        last = mm(ps_x[:, 0, b * 2 * H:(b + 1) * 2 * H], ht[p.e][:, c, b * P:(b + 1) * P],
                                  wa[:, c, :, :].rearrange("p j h -> p (j h)"), c == 0, c == C - 1)
                last.then_inc(S["cols_done"], 1)

            def score_rows(p):
                wait(pe, "cols_copied", p)
                wait_bank(p, ("result_ready", 1, 4), ("cols_copied", 1, 0))
                pe.transpose(ps_x[:, 0, 0:P], f_rep[p.e][:, :], ident[:, :]).then_inc(S["rows_done"], 1)

            def scores(p, b):
                if p.is_first() and b == 0:
                    pe.wait_ge(rowsel_ready, 3)
                wait(pe, "rows_third", p)
                f1, f2 = b * 2 * H, b * 2 * H + H
                mm(ps_x[:, b, :], f_parts[p.e][:, :], rowsel[:, f1:f1 + H, :].rearrange("p h m -> p (h m)"), True, False)
                for hd in range(H):
                    last = mm(ps_x[:, b, hd * P:(hd + 1) * P], rowsel[:, f2 + hd, :], f_parts[p.e][:, :], False, hd == H - 1)
                last.then_inc(S["scores_done"], 1)

            def prob_transposes(p, b):
                wait(pe, "probs_ready", p, b + 1)
                if b == 0:
                    wait_bank(p, ("gd_lo", 1, 3), ("scores_copied", 1, 0))
                if b == 1:
                    wait_bank(p, ("gd_lo", 2, 3), ("scores_copied", 2, 0))
                for hd in range(H):
                    last = pe.transpose(ps_x[:, b, hd * P:(hd + 1) * P], zn[:, b, hd, :], ident[:, :])
                last.then_inc(S["probs_transposed"], 1)

            def score_rows2(p):
                wait(pe, "wh2_scores_copied", p)
                wait_bank(p, ("normal2_ready", 2, 1))
                pe.transpose(ps_z[:, 0, 0:P], f2_rep[p.e][:, :], ident[:, :]).then_inc(S["rows2_done"], 1)

            def scores2(p):
                wait(pe, "rows2_third", p)
                wait_bank(p, ("ffn_plus_out", 2, 1))
                mm(ps_z[:, 1, 0:2 * P], ident_bf[:, :], mask_bf[:, :, :].rearrange("p b m -> p (b m)"), True, False)
                mm(ps_z[:, 1, 0:2 * P], g_parts[p.e][:, :], rowsel[:, 0:2, :].rearrange("p b m -> p (b m)"), False, False)
                for b in range(2):
                    last = mm(ps_z[:, 1, b * P:(b + 1) * P], rowsel[:, 2 + b, :], g_parts[p.e][:, :], False, b == 1)
                last.then_inc(S["scores2_done"], 1)

            def prob_transposes2(p):
                wait(pe, "probs2_ready", p)
                for b in range(2):
                    last = pe.transpose(ps_z[:, 0, b * P:(b + 1) * P], yn[p.e][:, b, :], ident[:, :])
                last.then_inc(S["probs2_transposed"], 1)

            def out2(p):
                wait(pe, "probs2_copied", p)
                wait(pe, "wh2_copied", p)
                for oc in range(C):
                    for b in range(2):
                        last = mm(ps_z[:, 1, (oc * 2 + b) * P:(oc * 2 + b + 1) * P],
                                  wh2[p.e][:, b, oc * P:(oc + 1) * P], a2t[p.e][:, b, :], True, True)
                last.then_inc(S["out_done"], 1)

            def hidden(p, dc):
                if p.is_first() and dc == 0:
                    pe.wait_ge(ffn_in, 32)
                wait(pe, "out_elu", p)
                for c in range(C):
                    last = mm(ps_z[:, 0, dc * 2 * P:(dc + 1) * 2 * P], w1_sb[:, c, dc * P:(dc + 1) * P],
                              ov[p.e][:, c, :], c == 0, c == C - 1)
                last.then_inc(S["hidden_done"], 1)

            def ffn(p, oc):
                wait(pe, "hidden_ready", p)
                for c in range(C):
                    last = mm(ps_z[:, 1, oc * 2 * P:(oc + 1) * 2 * P], w2_sb[:, c, oc * P:(oc + 1) * P],
                              hid[p.e][:, c, :], c == 0, c == C - 1)
                if oc == C - 1:
                    last.then_inc(S["ffn_done"], 1)

            def y_transposes(p):
                wait(pe, "ffn_plus_out", p)
                for b in range(2):
                    for oc in range(C):
                        last = pe.transpose(ps_z[:, 0, b * F + oc * P:b * F + (oc + 1) * P],
                                            ov[p.e][:, oc, b * P:(b + 1) * P], ident[:, :])
                    last.then_inc(S["ffn_transposed"], 1)

            def gather(p, b):
                wait(pe, "h3_lo", p)
                if b == 0:
                    wait_bank(p, ("scores_copied", 1, -3), ("result_ready", 1, 1))
                if b == 1:
                    wait_bank(p, ("scores_copied", 2, -3), ("at_lo", 2, -2), ("gd_lo", 2, 1))
                right = adj_deg[:, :, :].rearrange("p s n -> p (s n)")
                for c in range(C):
                    cols = slice(c * P, (c + 1) * P)
                    mm(ps_x[:, b, c * F:(c + 1) * F], h3_hi[:, b, cols], right, True, False)
                    last = mm(ps_x[:, b, c * F:(c + 1) * F], h3_lo[:, b, cols], right, False, True)
                last.then_inc(S["gather_done"], 1)

            def last_product(p, b, s):
                if b == s == 0:
                    wait(pe, "gd_lo", p)
                if b == 0 and s == 0:
                    wait_bank(p, ("cols_copied", 1, -4), ("at_lo", 1, -3), ("gd_lo", 1, 0))
                for c in range(C):
                    last = three(ps_x[:, 0, b * F:(b + 1) * F], (gd_hi[:, b, c, s, :], gd_lo[:, b, c, s, :]),
                                 (l1w_hi[:, 1 - s, c, :], l1w_lo[:, 1 - s, c, :]),
                                 s == 0 and c == 0, s == 1 and c == C - 1)
                if b == s == 1:
                    last.then_inc(S["last_done"], 1)

            def one(pairs):
                if p := pairs[4]:
                    hidden(p, 1)
                if p := pairs[3]:
                    h2_unit(p, 3, 1)
                if p := pairs[5]:
                    gather(p, 1)
                if p := pairs[4]:
                    ffn(p, 0)
                    ffn(p, 1)
                if p := pairs[2]:
                    prob_transposes(p, 0)
                if p := pairs[3]:
                    wh2_part(p, 0, 0)
                    wh2_part(p, 0, 1)
                if p := pairs[4]:
                    y_transposes(p)
                if p := pairs[3]:
                    wh2_part(p, 0, 2)
                if p := pairs[2]:
                    gh_unit(p, 0)
                    gh_unit(p, 1)
                if p := pairs[3]:
                    wh2_part(p, 0, 3)
                    wh2_part(p, 1, 0)
                if p := pairs[2]:
                    prob_transposes(p, 1)
                if p := pairs[3]:
                    wh2_part(p, 1, 1)
                    wh2_part(p, 1, 2)
                    wh2_part(p, 1, 3)
                if p := pairs[1]:
                    h_transposes(p)
                if p := pairs[2]:
                    gh_unit(p, 2)
                if p := pairs[3]:
                    score_rows2(p)
                if p := pairs[1]:
                    score_cols(p)
                if p := pairs[2]:
                    gh_unit(p, 3)
                if p := pairs[5]:
                    last_product(p, 0, 0)
                    last_product(p, 0, 1)
                if p := pairs[3]:
                    scores2(p)
                if p := pairs[5]:
                    last_product(p, 1, 0)
                    last_product(p, 1, 1)
                if p := pairs[2]:
                    h2_unit(p, 0, 0)
                    h2_unit(p, 0, 1)
                if p := pairs[1]:
                    score_rows(p)
                if p := pairs[2]:
                    h2_unit(p, 1, 0)
                if p := pairs[3]:
                    prob_transposes2(p)
                if p := pairs[2]:
                    h2_unit(p, 1, 1)
                if p := pairs[1]:
                    scores(p, 0)
                if p := pairs[3]:
                    out2(p)
                if p := pairs[1]:
                    scores(p, 1)
                if p := pairs[4]:
                    gather(p, 0)
                if p := pairs[2]:
                    h2_unit(p, 2, 0)
                    h2_unit(p, 2, 1)
                    h2_unit(p, 3, 0)
                if p := pairs[3]:
                    hidden(p, 0)
            steps(pe, one, [no_setup, no_setup, later_weights])


NAMES = ["x", "adj", "L0_gnn_W_heads", "L0_gnn_a_heads", "L0_gnn_W_out", "L0_gnn_a_out", "L0_gnn_w1", "L0_gnn_b1",
         "L0_gnn_w2", "L0_gnn_b2", "L0_gnn_ln_gamma", "L0_gnn_ln_beta", "L1_gnn_W", "L1_gnn_b"]


def kernel(**inputs):
    import concourse.bacc as bacc
    from concourse.bass_utils import run_bass_kernel_spmd

    nc = bacc.Bacc("TRN2", target_bir_lowering=False, num_devices=1)
    arrays, args = {}, []
    for name in NAMES:
        a = np.ascontiguousarray(inputs[name])
        arrays[f"in_{name}"] = a
        args.append(nc.dram_tensor(f"in_{name}", a.shape, mybir.dt.from_np(a.dtype), kind="ExternalInput").ap())
    args.append(nc.dram_tensor("out_0", (BATCH, P, F), F32, kind="ExternalOutput").ap())
    build(nc, *args)
    r = run_bass_kernel_spmd(nc, [arrays], core_ids=[0])
    return r.results[0]["out_0"]
```
